# Optimizing a Trainium2 kernel written in Bass

```python
import numpy as np
import jax
import jax.numpy as jnp

def _softmax(x, axis=-1):
    return jax.nn.softmax(x, axis=axis)

def _gelu(x):
    return jax.nn.gelu(x, approximate=True)

def _silu(x):
    return jax.nn.silu(x)

def _sigmoid(x):
    return jax.nn.sigmoid(x)

def _layernorm(x, axis=-1, eps=1e-05):
    m = jnp.mean(x, axis=axis, keepdims=True)
    v = jnp.var(x, axis=axis, keepdims=True)
    return (x - m) / jnp.sqrt(v + eps)

def _scatter_add(tgt, idx, src, axis=0):
    return tgt.at[idx].add(src)

def _segment_sum(src, seg, n):
    return jax.ops.segment_sum(src, seg, n)
kernel_name = 'mk_gnn_preln_d1_gnn_r32_bf7e59'

def setup_inputs(seed: int=0):
    np.random.seed(seed)
    _w = jnp.asarray

    def _rec_inputs():
        import jax
        import jax.numpy as jnp
        _gk = jax.random.key(seed)
        x = -0.000202 + 1 * jax.random.normal(jax.random.fold_in(_gk, 1), (3125, 128), jnp.float32)
        _s = jax.random.randint(jax.random.fold_in(_gk, 2), (50000,), 0, 3125, jnp.int32)
        _d = jax.random.randint(jax.random.fold_in(_gk, 3), (50000,), 0, 3125, jnp.int32)
        _loop = jnp.arange(3125, dtype=jnp.int32)
        src = jnp.concatenate([_s, _d, _loop])
        dst = jnp.concatenate([_d, _s, _loop])
        _o = jnp.argsort(dst, stable=True)
        src = src[_o]
        dst = dst[_o]
        return (x, src, dst)
    x, src, dst = _rec_inputs()

    def _L0_gnn_setup():
        import jax, jax.numpy as jnp
        import numpy as np
        N, E, D, H, L, FF = (50000, 15625, 128, 8, 2, 512)
        HD = D // H

        def _layernorm(x, g, b):
            mu = jnp.mean(x, axis=-1, keepdims=True)
            var = jnp.mean(jnp.square(x - mu), axis=-1, keepdims=True)
            return (x - mu) * jax.lax.rsqrt(var + 1e-05) * g + b

        def _forward(edge_index, x, Wq, bq, Wk, bk, Wv, bv, Wo, bo, Wpos, bpos, Wdeg, bdeg, ln1_g, ln1_b, ln2_g, ln2_b, W1, b1, W2, b2):
            n = x.shape[0]
            loops = jnp.arange(n, dtype=edge_index.dtype)
            src = jnp.concatenate([edge_index[0], loops])
            dst = jnp.concatenate([edge_index[1], loops])
            scale = np.float32(np.sqrt(HD))
            for l in range(L):
                xn = _layernorm(x, ln1_g[l], ln1_b[l])
                deg = jax.ops.segment_sum(jnp.ones_like(src, dtype=x.dtype), src, num_segments=n)
                deg = (deg - deg.mean()) / (jnp.std(deg, ddof=1) + 1e-06)
                pos = xn @ Wpos[l] + bpos[l] + deg[:, None] * Wdeg[l][0] + bdeg[l]
                xp = xn + pos
                q = (xp @ Wq[l] + bq[l]).reshape(n, H, HD)
                k = (xp @ Wk[l] + bk[l]).reshape(n, H, HD)
                v = (xp @ Wv[l] + bv[l]).reshape(n, H, HD)
                att = jnp.einsum('ehd,ehd->eh', q[dst], k[src]) / scale
                att = jnp.nan_to_num(jnp.clip(att, -50.0, 50.0), nan=0.0, posinf=50.0, neginf=-50.0)
                m = jax.ops.segment_max(att, dst, num_segments=n)
                ex = jnp.exp(att - m[dst])
                s = jax.ops.segment_sum(ex, dst, num_segments=n)
                alpha = ex / (s[dst] + 1e-16)
                msg = (v[src] * alpha[:, :, None]).reshape(-1, D)
                aggr = jax.ops.segment_sum(msg, dst, num_segments=n)
                x = x + (aggr @ Wo[l] + bo[l])
                h = jax.nn.gelu(_layernorm(x, ln2_g[l], ln2_b[l]) @ W1[l] + b1[l], approximate=False)
                x = x + (h @ W2[l] + b2[l])
            return x
        key = jax.random.key(seed)
        ks = jax.random.split(key, 16)
        inp = {'x': jax.random.normal(ks[0], (N, D), jnp.float32), 'edge_index': jax.random.randint(ks[1], (2, E), 0, N, jnp.int32)}

        def w(k, shape, fan_in):
            return jax.random.normal(k, shape, jnp.float32) / np.float32(np.sqrt(fan_in))
        inp['Wq'] = w(ks[2], (L, D, D), D)
        inp['Wk'] = w(ks[3], (L, D, D), D)
        inp['Wv'] = w(ks[4], (L, D, D), D)
        inp['Wo'] = w(ks[5], (L, D, D), D)
        inp['Wpos'] = w(ks[6], (L, D, D), D)
        inp['Wdeg'] = w(ks[7], (L, 1, D), 1)
        inp['W1'] = w(ks[8], (L, D, FF), D)
        inp['W2'] = w(ks[9], (L, FF, D), FF)
        for name, shape in [('bq', (L, D)), ('bk', (L, D)), ('bv', (L, D)), ('bo', (L, D)), ('bpos', (L, D)), ('bdeg', (L, D)), ('ln1_b', (L, D)), ('ln2_b', (L, D)), ('b1', (L, FF)), ('b2', (L, D))]:
            inp[name] = jnp.zeros(shape, jnp.float32)
        inp['ln1_g'] = jnp.ones((L, D), jnp.float32)
        inp['ln2_g'] = jnp.ones((L, D), jnp.float32)
        return inp
    _L0_gnn_all = _L0_gnn_setup()
    _L0_gnn_in = {k: v for k, v in _L0_gnn_all.items() if k in ('Wq', 'bq', 'Wk', 'bk', 'Wv', 'bv', 'Wo', 'bo', 'Wpos', 'bpos', 'Wdeg', 'bdeg', 'ln1_g', 'ln1_b', 'ln2_g', 'ln2_b', 'W1', 'b1', 'W2', 'b2')}
    del _L0_gnn_all
    return {'x': x, 'src': src, 'dst': dst, 'L0_gnn_Wq': _L0_gnn_in['Wq'], 'L0_gnn_bq': _L0_gnn_in['bq'], 'L0_gnn_Wk': _L0_gnn_in['Wk'], 'L0_gnn_bk': _L0_gnn_in['bk'], 'L0_gnn_Wv': _L0_gnn_in['Wv'], 'L0_gnn_bv': _L0_gnn_in['bv'], 'L0_gnn_Wo': _L0_gnn_in['Wo'], 'L0_gnn_bo': _L0_gnn_in['bo'], 'L0_gnn_Wpos': _L0_gnn_in['Wpos'], 'L0_gnn_bpos': _L0_gnn_in['bpos'], 'L0_gnn_Wdeg': _L0_gnn_in['Wdeg'], 'L0_gnn_bdeg': _L0_gnn_in['bdeg'], 'L0_gnn_ln1_g': _L0_gnn_in['ln1_g'], 'L0_gnn_ln1_b': _L0_gnn_in['ln1_b'], 'L0_gnn_ln2_g': _L0_gnn_in['ln2_g'], 'L0_gnn_ln2_b': _L0_gnn_in['ln2_b'], 'L0_gnn_W1': _L0_gnn_in['W1'], 'L0_gnn_b1': _L0_gnn_in['b1'], 'L0_gnn_W2': _L0_gnn_in['W2'], 'L0_gnn_b2': _L0_gnn_in['b2']}

def reference(x, src, dst, L0_gnn_Wq, L0_gnn_bq, L0_gnn_Wk, L0_gnn_bk, L0_gnn_Wv, L0_gnn_bv, L0_gnn_Wo, L0_gnn_bo, L0_gnn_Wpos, L0_gnn_bpos, L0_gnn_Wdeg, L0_gnn_bdeg, L0_gnn_ln1_g, L0_gnn_ln1_b, L0_gnn_ln2_g, L0_gnn_ln2_b, L0_gnn_W1, L0_gnn_b1, L0_gnn_W2, L0_gnn_b2):
    import jax
    import jax.numpy as jnp

    def _L0_gnn_ref(x, edge_index, Wq, bq, Wk, bk, Wv, bv, Wo, bo, Wpos, bpos, Wdeg, bdeg, ln1_g, ln1_b, ln2_g, ln2_b, W1, b1, W2, b2):
        import jax, jax.numpy as jnp
        import numpy as np
        N, E, D, H, L, FF = (50000, 15625, 128, 8, 2, 512)
        HD = D // H

        def _layernorm(x, g, b):
            mu = jnp.mean(x, axis=-1, keepdims=True)
            var = jnp.mean(jnp.square(x - mu), axis=-1, keepdims=True)
            return (x - mu) * jax.lax.rsqrt(var + 1e-05) * g + b

        def _forward(edge_index, x, Wq, bq, Wk, bk, Wv, bv, Wo, bo, Wpos, bpos, Wdeg, bdeg, ln1_g, ln1_b, ln2_g, ln2_b, W1, b1, W2, b2):
            n = x.shape[0]
            loops = jnp.arange(n, dtype=edge_index.dtype)
            src = jnp.concatenate([edge_index[0], loops])
            dst = jnp.concatenate([edge_index[1], loops])
            scale = np.float32(np.sqrt(HD))
            for l in range(L):
                xn = _layernorm(x, ln1_g[l], ln1_b[l])
                deg = jax.ops.segment_sum(jnp.ones_like(src, dtype=x.dtype), src, num_segments=n)
                deg = (deg - deg.mean()) / (jnp.std(deg, ddof=1) + 1e-06)
                pos = xn @ Wpos[l] + bpos[l] + deg[:, None] * Wdeg[l][0] + bdeg[l]
                xp = xn + pos
                q = (xp @ Wq[l] + bq[l]).reshape(n, H, HD)
                k = (xp @ Wk[l] + bk[l]).reshape(n, H, HD)
                v = (xp @ Wv[l] + bv[l]).reshape(n, H, HD)
                att = jnp.einsum('ehd,ehd->eh', q[dst], k[src]) / scale
                att = jnp.nan_to_num(jnp.clip(att, -50.0, 50.0), nan=0.0, posinf=50.0, neginf=-50.0)
                m = jax.ops.segment_max(att, dst, num_segments=n)
                ex = jnp.exp(att - m[dst])
                s = jax.ops.segment_sum(ex, dst, num_segments=n)
                alpha = ex / (s[dst] + 1e-16)
                msg = (v[src] * alpha[:, :, None]).reshape(-1, D)
                aggr = jax.ops.segment_sum(msg, dst, num_segments=n)
                x = x + (aggr @ Wo[l] + bo[l])
                h = jax.nn.gelu(_layernorm(x, ln2_g[l], ln2_b[l]) @ W1[l] + b1[l], approximate=False)
                x = x + (h @ W2[l] + b2[l])
            return x
        return _forward(edge_index, x, Wq, bq, Wk, bk, Wv, bv, Wo, bo, Wpos, bpos, Wdeg, bdeg, ln1_g, ln1_b, ln2_g, ln2_b, W1, b1, W2, b2)
    edge_index = jnp.stack([src, dst])
    h = jnp.maximum(_layernorm(x, axis=-1), 0.0)
    x = x + _L0_gnn_ref(h, edge_index, L0_gnn_Wq, L0_gnn_bq, L0_gnn_Wk, L0_gnn_bk, L0_gnn_Wv, L0_gnn_bv, L0_gnn_Wo, L0_gnn_bo, L0_gnn_Wpos, L0_gnn_bpos, L0_gnn_Wdeg, L0_gnn_bdeg, L0_gnn_ln1_g, L0_gnn_ln1_b, L0_gnn_ln2_g, L0_gnn_ln2_b, L0_gnn_W1, L0_gnn_b1, L0_gnn_W2, L0_gnn_b2)
    return x

_drawn_inputs = setup_inputs


def setup_inputs(seed=0):
    import zlib

    import numpy as np

    out = dict(_drawn_inputs(seed))
    spreads = {'L0_gnn_bq': (0.0, 0.1),
     'L0_gnn_bk': (0.0, 0.1),
     'L0_gnn_bv': (0.0, 0.1),
     'L0_gnn_bo': (0.0, 0.1),
     'L0_gnn_bpos': (0.0, 0.1),
     'L0_gnn_bdeg': (0.0, 0.1),
     'L0_gnn_ln1_g': (1.0, 0.2),
     'L0_gnn_ln1_b': (0.0, 0.1),
     'L0_gnn_ln2_g': (1.0, 0.2),
     'L0_gnn_ln2_b': (0.0, 0.1),
     'L0_gnn_b1': (0.0, 0.1),
     'L0_gnn_b2': (0.0, 0.1)}
    factors = {}
    for name, (base, spread) in spreads.items():
        noise = np.random.default_rng([zlib.crc32(name.encode()), seed]).standard_normal(out[name].shape)
        drawn = base * np.exp(spread * noise) if base else spread * noise
        out[name] = jnp.asarray(drawn.astype(out[name].dtype))
    for name, factor in factors.items():
        out[name] = (out[name] * factor).astype(out[name].dtype)
    return out
```

```python
from contextlib import ExitStack

import numpy as np

import concourse.bass as bass
from concourse import mybir

F32 = mybir.dt.float32
BF16 = mybir.dt.bfloat16
I32 = mybir.dt.int32
U32 = mybir.dt.uint32
U8 = mybir.dt.uint8
ALU = mybir.AluOpType
ACT = mybir.ActivationFunctionType
AX = mybir.AxisListType.X
ENG = mybir.EngineType

P = 128
N, D, H, L, FF = 3125, 128, 8, 2, 512
HD = D // H
E = 103125
BLOCKS = -(-N // P)
NP = BLOCKS * P
TAIL = N - (BLOCKS - 1) * P
TILES = -(-E // P)
G = 4
RING = 4
STEPS = TILES - 1 + BLOCKS
ROUNDS = -(-STEPS // (G * RING))
GROUPS = ROUNDS * RING
STEPS_P = GROUPS * G
TILES_P = STEPS_P - (BLOCKS - 1)
SC = -(-(STEPS_P + G * RING) // P)
TC = -(-TILES_P // P)
FC = FF // P
CONSTS = 14
KV = 2 * D
AGG = D + H
CB = 4
CHUNKS = [(c * CB, min(CB, BLOCKS - c * CB)) for c in range(-(-BLOCKS // CB))]
NCH = len(CHUNKS)
HT = 8
HSTEPS = TILES_P // HT
W_POS, W_QKV, W_O, W_1, W_2 = 0, D, 4 * D, 5 * D, 5 * D + FF
W_COLS = W_2 + FC * D
V_G1, V_B1, V_G2, V_B2, V_POS, V_DEG, V_FF = range(W_COLS, W_COLS + 7)
W_ALL = V_FF + FC
R_QKV, R_O, R_2 = 0, 3 * D, 4 * D
R_ALL = 5 * D


def given(g, low, high=GROUPS * L * G):
    return not isinstance(g, int) or low <= g < high


def build(nc, x_in, src_tiles, dst_tiles, dst_last, weights, rows, wdeg_in, out):
    with ExitStack() as ctx:
        def sb(name, shape, dt=F32):
            return ctx.enter_context(nc.sbuf_tensor(name, shape, dt))

        def sem(name):
            return ctx.enter_context(nc.semaphore(name))

        bank = [ctx.enter_context(nc.psum_tensor(f"bank{i}", [P, 512], F32)) for i in range(8)]

        kv_table = [nc.dram_tensor(f"kv_table{l}", [NP, KV], F32, kind="Internal").ap() for l in range(L)]
        block_dram = nc.dram_tensor("block_dram", [SC * P], I32, kind="Internal").ap()
        deg_dram = nc.dram_tensor("deg_dram", [NP], F32, kind="Internal").ap()

        iota_free = sb("iota_free", [P, P])
        iota_bf = sb("iota_bf", [P, P], BF16)
        ones = sb("ones", [P, P])
        ident = sb("ident", [P, P])
        ident_bf = sb("ident_bf", [P, P], BF16)
        eps = sb("eps", [P, 1])
        zeros = sb("zeros", [P, BLOCKS * H])
        valid = sb("valid", [P, BLOCKS])
        w = [sb(f"w{l}", [P, W_ALL]) for l in range(L)]
        row = [sb(f"row{l}", [P, R_ALL]) for l in range(L)]
        wdeg = sb("wdeg", [1, L, D])
        pos_bias = sb("pos_bias", [P, L])
        x0 = sb("x0", [P, BLOCKS, D])
        x = sb("x", [P, BLOCKS, D])
        xn = sb("xn", [P, BLOCKS, D])
        xnT = sb("xnT", [P, NP])
        qkv = sb("qkv", [P, BLOCKS, 3 * D])
        qp = sb("qp", [P, BLOCKS, 3, D], BF16)
        qres = sb("qres", [P, 2, CB, D])
        agg = sb("agg", [P, BLOCKS, AGG])
        stats = sb("stats", [P, BLOCKS, 6])
        mv = sb("mv", [P, BLOCKS, 2])
        std = sb("std", [P, BLOCKS])
        rstd = sb("rstd", [P, BLOCKS])
        loop_att = sb("loop_att", [P, BLOCKS * H])
        loop_nan = sb("loop_nan", [P, BLOCKS * H], U8)
        rsum = sb("rsum", [P, BLOCKS, H])
        degrow = sb("degrow", [1, NP])
        rel = sb("rel", [P, SC * P])
        srcidx = sb("srcidx", [P, SC * P], U32)
        blockrow = sb("blockrow", [1, SC * P], I32)
        idx = sb("idx", [P, RING, G], U32)
        kvr = sb("kvr", [P, RING, G, KV])
        onehot = sb("onehot", [P, RING, G, P])
        onehotT = sb("onehotT", [P, 2, G, P], BF16)
        prod = sb("prod", [P, G, D])
        att = sb("att", [P, 2, G * H])
        attc = sb("attc", [P, 2, G * H])
        attnan = sb("attnan", [P, 2, G * H], U8)
        msg = sb("msg", [P, 2, G, AGG])
        last_i = sb("last_i", [P, TC], I32)
        last_f = sb("last_f", [P, TC])
        thr = sb("thr", [P, BLOCKS - 1])
        blockno = sb("blockno", [P, BLOCKS - 1])
        before = sb("before", [P, BLOCKS - 1, TC])
        count = sb("count", [P, BLOCKS - 1])
        first = sb("first", [P, BLOCKS - 1])
        stepno = sb("stepno", [P, SC])
        begun = sb("begun", [P, SC, BLOCKS - 1])
        block = sb("block", [P, SC])
        block128 = sb("block128", [P, SC])
        tileno = sb("tileno", [P, SC], U32)
        blockT = sb("blockT", [SC, P], I32)
        deg = sb("deg", [P, BLOCKS])
        degsq = sb("degsq", [P, BLOCKS])
        degsum = sb("degsum", [P, 1])
        degstd = sb("degstd", [P, 1])
        degT = sb("degT", [BLOCKS, P])
        hT = qkv[:].rearrange("p b c -> p (b c)")[:, 0:2 * FC * 512].rearrange("p (u f n) -> p u f n", u=2, f=FC)
        src_nat = xnT[:, 0:TILES_P].bitcast(I32)
        part_i = xnT[:, TILES_P:2 * TILES_P].bitcast(I32)
        lo = xnT[:, 2 * TILES_P:3 * TILES_P]
        step_dst = kvr[:].rearrange("p r g c -> p (r g c)")[:, 0:SC * P].bitcast(I32)
        step_src = kvr[:].rearrange("p r g c -> p (r g c)")[:, SC * P:2 * SC * P].bitcast(I32)
        xn_flat = xn[:].rearrange("p b c -> p (b c)")
        step_dst_f = xn_flat[:, 0:SC * P]
        step_src_f = xn_flat[:, SC * P:2 * SC * P]
        hi = xn_flat[:, 2 * SC * P:2 * SC * P + TILES_P // 2].bitcast(BF16)
        agg_bf = agg[:].rearrange("p b c -> p (b c)").bitcast(BF16)
        oh_lo = agg_bf[:, 0:2 * HT * P].rearrange("p (u j n) -> p u j n", u=2, j=HT)
        oh_hi = agg_bf[:, 2 * HT * P:2 * HT * (P + BLOCKS)].rearrange("p (u j n) -> p u j n", u=2, j=HT)

        s_x = sem("s_x")
        s_last = sem("s_last")
        s_src = sem("s_src")
        s_w = sem("s_w")
        s_const = sem("s_const")
        s_chain = sem("s_chain")
        s_count = sem("s_count")
        s_first_ps = sem("s_first_ps")
        s_block = sem("s_block")
        s_blockT_ps = sem("s_blockT_ps")
        s_blockT = sem("s_blockT")
        s_blockrow = sem("s_blockrow")
        s_tileno = sem("s_tileno")
        s_rows = sem("s_rows")
        s_rows_f = sem("s_rows_f")
        s_rowsT_ps = sem("s_rowsT_ps")
        s_rowsT = sem("s_rowsT")
        s_digits = sem("s_digits")
        s_hist_oh = sem("s_hist_oh")
        s_hist_mm = sem("s_hist_mm")
        s_degsum = sem("s_degsum")
        s_degsum_ps = sem("s_degsum_ps")
        s_degstd = sem("s_degstd")
        s_deg = sem("s_deg")
        s_degT_ps = sem("s_degT_ps")
        s_degT = sem("s_degT")
        s_degrow = sem("s_degrow")
        s_stats = sem("s_stats")
        s_var = sem("s_var")
        s_std = sem("s_std")
        s_rstd = sem("s_rstd")
        s_xn = sem("s_xn")
        s_tp = sem("s_tp")
        s_xnT = sem("s_xnT")
        s_xp_ps = sem("s_xp_ps")
        s_xpT = sem("s_xpT")
        s_qkv_ps = sem("s_qkv_ps")
        s_qkv = sem("s_qkv")
        s_q1 = sem("s_q1")
        s_r1 = sem("s_r1")
        s_q2 = sem("s_q2")
        s_q3 = sem("s_q3")
        s_table = sem("s_table")
        s_loop_att = sem("s_loop_att")
        s_loop_ex = sem("s_loop_ex")
        s_agg0 = sem("s_agg0")
        s_rsum = sem("s_rsum")
        s_norm = sem("s_norm")
        s_o_ps = sem("s_o_ps")
        s_o = sem("s_o")
        s_ff1 = sem("s_ff1")
        s_gelu = sem("s_gelu")
        s_y_ps = sem("s_y_ps")
        s_y = sem("s_y")
        s_bias = sem("s_bias")
        s_final = sem("s_final")
        s_out = sem("s_out")
        s_idx = [sem(f"s_idx{r}") for r in range(RING)]
        s_kv = [sem(f"s_kv{r}") for r in range(RING)]
        s_seen = sem("s_seen")
        s_oh = sem("s_oh")
        s_ohT_ps = sem("s_ohT_ps")
        s_ohT = sem("s_ohT")
        s_qe = sem("s_qe")
        s_prod = sem("s_prod")
        s_att = sem("s_att")
        s_clip = sem("s_clip")
        s_attc = sem("s_attc")
        s_ex = sem("s_ex")
        s_msg = sem("s_msg")
        s_agg_ps = sem("s_agg_ps")
        s_agg = sem("s_agg")

        def chunk_cols(c):
            b0, nb = CHUNKS[c]
            return slice(b0 * P, (b0 + nb) * P)

        def chunk_bank(i, c):
            return bank[i][:, 0:CHUNKS[c][1] * D].rearrange("p (b c) -> p b c", c=D)

        def chunk_blocks(t, c):
            b0, nb = CHUNKS[c]
            return t[:, b0:b0 + nb, :]

        def tp_no(l, phase, c):
            return (l * 3 + phase) * NCH + c

        def xn_no(n, c):
            return n * BLOCKS + CHUNKS[c][0] + CHUNKS[c][1]

        def agg_bank(r, j):
            return bank[4 + 2 * (r % 2) + j // 2][:, j % 2 * AGG:(j % 2 + 1) * AGG]

        def read_blocks(engine, g):
            return nc.values_load_multi_w_load_instructions(blockrow[0:1, bass.ds(g * G, G)], engines=(engine,), min_val=0, max_val=BLOCKS - 1,
                                                             skip_runtime_bounds_check_because="a count of the blocks after the first")[1]

        program = ctx.enter_context(nc.Block())

        @program.sync
        def _(sp):
            sp.dma_start(last_i[:], dst_last).then_inc(s_last, 16)
            sp.dma_start(src_nat, src_tiles.rearrange("t e -> (t e)").rearrange("(p t) -> p t", p=P)).then_inc(s_src, 16)
            sp.dma_start(x0[:], x_in.rearrange("(b p) c -> p b c", p=P)).then_inc(s_x, 16)
            for l in range(L):
                sp.dma_start(w[l][:], weights[l]).then_inc(s_w, 16)
                sp.dma_start(row[l][:], rows[l:l + 1, :].broadcast_to([P, R_ALL])).then_inc(s_w, 16)
            sp.dma_start(wdeg[:], wdeg_in).then_inc(s_w, 16)
            sp.wait_ge(s_blockT, 1)
            sp.dma_start(block_dram.rearrange("(c i) -> c i", i=P), blockT[:]).then_inc(s_blockrow, 16)
            sp.wait_ge(s_blockrow, 16)
            sp.dma_start(blockrow[:], block_dram.rearrange("(a i) -> a i", a=1)).then_inc(s_blockrow, 16)
            sp.wait_ge(s_degT, 1)
            sp.dma_start(deg_dram.rearrange("(b i) -> b i", i=P), degT[:]).then_inc(s_degrow, 16)
            sp.wait_ge(s_degrow, 16)
            sp.dma_start(degrow[:], deg_dram.rearrange("(a i) -> a i", a=1)).then_inc(s_degrow, 16)
            for l in range(L):
                table = kv_table[l].rearrange("(b p) c -> p b c", p=P)
                for c, (b0, nb) in enumerate(CHUNKS):
                    sp.wait_ge(s_qkv, l * BLOCKS + b0 + nb)
                    sp.dma_start(table[:, b0:b0 + nb, :], qkv[:, b0:b0 + nb, D:3 * D]).then_inc(s_table, 16)
            for c, (b0, nb) in enumerate(CHUNKS):
                sp.wait_ge(s_final, c + 1)
                if b0 + nb < BLOCKS:
                    sp.dma_start(out[b0 * P:(b0 + nb) * P, :].rearrange("(b p) c -> p b c", p=P), x0[:, b0:b0 + nb, :]).then_inc(s_out, 16)
                else:
                    sp.dma_start(out[b0 * P:N, :], x0[0:TAIL, b0, :]).then_inc(s_out, 16)
            sp.wait_ge(s_out, 16 * NCH)

        @program.gpsimd
        def _(pool):
            def iota(t, pattern, base, per_partition=0):
                pool.iota(t[:], pattern, base=base, channel_multiplier=per_partition, allow_small_or_imprecise_dtypes=True).then_inc(s_const, 1)

            iota(thr, [[P, BLOCKS - 1]], P)
            iota(blockno, [[1, BLOCKS - 1]], 1)
            iota(stepno, [[P, SC]], 0, 1)
            iota(iota_free, [[1, P]], 0)
            iota(iota_bf, [[1, P]], 0)
            for t, value in ((ones, 1.0), (ident, 0.0), (ident_bf, 0.0), (valid, 1.0), (eps, 1e-5), (zeros, 0.0)):
                pool.memset(t[:], value).then_inc(s_const, 1)
            pool.wait_ge(s_const, 11)
            pool.affine_select(out=ident[:], in_=ident[:], compare_op=ALU.not_equal, fill=1.0, base=0, pattern=[[-1, P]], channel_multiplier=1).then_inc(s_const, 1)
            pool.affine_select(out=ident_bf[:], in_=ident_bf[:], compare_op=ALU.not_equal, fill=1.0, base=0, pattern=[[-1, P]], channel_multiplier=1).then_inc(s_const, 1)
            pool.affine_select(out=valid[:], in_=valid[:], compare_op=ALU.is_ge, fill=0.0, base=N - 1, pattern=[[-P, BLOCKS]], channel_multiplier=-1).then_inc(s_const, 1)
            pool.wait_ge(s_tileno, 1)
            for rows_of, tiles in ((step_dst, dst_tiles), (step_src, src_tiles)):
                for c in range(SC):
                    pool.indirect_dma_start(rows_of[:, c * P:(c + 1) * P], None, tiles, bass.IndirectOffsetOnAxis(ap=tileno[:, c:c + 1], axis=0)).then_inc(s_rows, 16)

            for l in range(L):
                pool.wait_ge(s_table, 16 * NCH * (l + 1))
                with pool.Fori(0, ROUNDS) as it:
                    for r in range(RING):
                        pool.wait_ge(s_idx[r], it + (l * ROUNDS + 1))
                        pool.sem_inc(s_seen, 1)
                        for j in range(G):
                            pool.indirect_dma_start(kvr[:, r, j, :], None, kv_table[l], bass.IndirectOffsetOnAxis(ap=idx[:, r, j:j + 1], axis=0)).then_inc(s_kv[r], 16)

        @program.tensor
        def _(pe):
            pe.wait_ge(s_const, CONSTS)
            pe.wait_ge(s_count, 1)
            pe.matmul(bank[0][:, 0:BLOCKS - 1], ones[:], count[:], start=True, stop=True).then_inc(s_first_ps, 1)
            pe.wait_ge(s_block, 1)
            pe.transpose(bank[1][0:SC, 0:P], block[:], ident[:]).then_inc(s_blockT_ps, 1)

            def hist_step(k, buf, start=False, stop=False):
                pe.wait_ge(s_hist_oh, k + 1)
                for j in range(HT):
                    mm = pe.matmul(bank[2][:, 0:BLOCKS], oh_lo[:, buf, j, :], oh_hi[:, buf, j, :], start=start and j == 0, stop=stop and j == HT - 1)
                mm.then_inc(s_hist_mm, 1)

            hist_step(0, 0, start=True)
            with pe.Fori(0, HSTEPS // 2 - 1) as i:
                hist_step(2 * i + 1, 1)
                hist_step(2 * i + 2, 0)
            for k in range(2 * (HSTEPS // 2) - 1, HSTEPS):
                hist_step(k, k % 2, stop=k == HSTEPS - 1)

            pe.wait_ge(s_degsum, 1)
            pe.matmul(bank[0][:, 0:1], ones[:], degsum[:], start=True, stop=True).then_inc(s_degsum_ps, 1)
            pe.wait_ge(s_deg, 1)
            pe.transpose(bank[1][0:BLOCKS, 0:P], deg[:], ident[:]).then_inc(s_degT_ps, 1)
            for k in range(2 * SC):
                pe.wait_ge(s_rows_f, k + 1)
                if k >= 2:
                    pe.wait_ge(s_rowsT, k - 1)
                rows_f = step_dst_f if k < SC else step_src_f
                pe.transpose(bank[3 + k % 2][:, 0:P], rows_f[:, k % SC * P:(k % SC + 1) * P], ident[:]).then_inc(s_rowsT_ps, 1)

            def turn(l, phase, c, n=None):
                if n is None:
                    pe.wait_ge(s_norm, l * NCH + c + 1)
                else:
                    pe.wait_ge(s_xn, xn_no(n, c))
                t = tp_no(l, phase, c)
                if t >= 2:
                    pe.wait_ge(s_xnT, t - 1)
                b0, nb = CHUNKS[c]
                for b in range(nb):
                    mm = pe.transpose(bank[t % 2][:, b * P:(b + 1) * P], xn[:, b0 + b, :], ident[:])
                mm.then_inc(s_tp, 1)

            def pos(l, c):
                pe.wait_ge(s_xnT, tp_no(l, 0, c) + 1)
                if c >= 2:
                    pe.wait_ge(s_xpT, l * NCH + c - 1)
                o = bank[2 + c % 2][:, 0:CHUNKS[c][1] * P]
                pe.matmul(o, w[l][:, W_POS:W_POS + D], xnT[:, chunk_cols(c)], start=True, stop=False)
                pe.matmul(o, wdeg[0:1, l, :], degrow[0:1, chunk_cols(c)], start=False, stop=True).then_inc(s_xp_ps, 1)

            def project(l, c):
                pe.wait_ge(s_xpT, l * NCH + c + 1)
                b0, nb = CHUNKS[c]
                for b in range(b0, b0 + nb):
                    if b >= 4:
                        pe.wait_ge(s_qkv, l * BLOCKS + b - 3)
                    pe.matmul(bank[4 + b % 4][:, 0:3 * D], xnT[:, b * P:(b + 1) * P], w[l][:, W_QKV:W_QKV + 3 * D], start=True, stop=True).then_inc(s_qkv_ps, 1)

            def edge_turn(l, g, r):
                n = l * GROUPS + g
                pe.wait_ge(s_oh, n + 1)
                view = onehot[:, r, :, :].bitcast(BF16).rearrange("p j (n two) -> p j n two", two=2)
                for j in range(G):
                    mm = pe.transpose(bank[r % 2][:].bitcast(BF16)[:, j * P:(j + 1) * P], view[:, j, :, 1], ident_bf[:])
                mm.then_inc(s_ohT_ps, 1)

            def edge_q(l, g, r, blocks):
                n = l * GROUPS + g
                pe.wait_ge(s_ohT, n + 1)
                for j in range(G):
                    for part in range(3):
                        mm = pe.matmul(bank[2 + r % 2][:, j * D:(j + 1) * D], onehotT[:, r % 2, j, :],
                                       qp[:, bass.ds(blocks[j], 1), part, :].rearrange("p a c -> p (a c)"), start=part == 0, stop=part == 2)
                mm.then_inc(s_qe, 1)

            def edge_sum(l, g, r):
                n = l * GROUPS + g
                pe.wait_ge(s_msg, n + 1)
                for j in range(G):
                    mm = pe.matmul(agg_bank(r, j), onehot[:, r, j, :], msg[:, r % 2, j, :], start=True, stop=True)
                mm.then_inc(s_agg_ps, 1)

            def edge_iteration(l, g, r):
                if given(g, 0, GROUPS - 1):
                    edge_q(l, g + 1, (r + 1) % RING, read_blocks(ENG.PE, g + 1))
                if given(g, 1):
                    edge_sum(l, g - 1, (r - 1) % RING)
                if given(g, 0, GROUPS - 2):
                    edge_turn(l, g + 2, (r + 2) % RING)

            def attention_out(l, c):
                pe.wait_ge(s_xnT, tp_no(l, 1, c) + 1)
                if c >= 2:
                    pe.wait_ge(s_o, l * NCH + c - 1)
                b0, nb = CHUNKS[c]
                for b in range(nb):
                    mm = pe.matmul(bank[2 + c % 2][:, b * D:(b + 1) * D], xnT[:, (b0 + b) * P:(b0 + b + 1) * P], w[l][:, W_O:W_O + D], start=True, stop=True)
                mm.then_inc(s_o_ps, 1)

            def hidden(l, c):
                pe.wait_ge(s_xnT, tp_no(l, 2, c) + 1)
                for f in range(FC):
                    if c >= 1:
                        pe.wait_ge(s_gelu, (l * NCH + c - 1) * FC + f + 1)
                    pe.matmul(bank[4 + f][:, 0:CHUNKS[c][1] * P], w[l][:, W_1 + f * P:W_1 + (f + 1) * P], xnT[:, chunk_cols(c)], start=True, stop=True).then_inc(s_ff1, 1)

            def ff_out(l, c):
                pe.wait_ge(s_gelu, (l * NCH + c + 1) * FC)
                if c >= 2:
                    pe.wait_ge(s_y, l * NCH + c - 1)
                for b in range(CHUNKS[c][1]):
                    for f in range(FC):
                        mm = pe.matmul(bank[2 + c % 2][:, b * D:(b + 1) * D], hT[:, c % 2, f, b * P:(b + 1) * P], w[l][:, W_2 + f * D:W_2 + (f + 1) * D], start=f == 0, stop=f == FC - 1)
                mm.then_inc(s_y_ps, 1)

            pe.wait_ge(s_w, 16 * (2 * L + 1))
            pe.wait_ge(s_degrow, 32)
            pe.wait_ge(s_blockrow, 32)
            for l in range(L):
                turn(l, 0, 0, n=2 * l + 1)
                for c in range(NCH):
                    if c + 1 < NCH:
                        turn(l, 0, c + 1, n=2 * l + 1)
                    pos(l, c)
                    if c >= 1:
                        project(l, c - 1)
                project(l, NCH - 1)

                pe.wait_ge(s_q3, (l + 1) * NCH)
                edge_turn(l, 0, 0)
                edge_turn(l, 1, 1)
                edge_q(l, 0, 0, read_blocks(ENG.PE, 0))
                for g in range(RING):
                    edge_iteration(l, g, g)
                with pe.Fori(1, ROUNDS - 1) as it:
                    for r in range(RING):
                        edge_iteration(l, it * RING + r, r)
                for r in range(RING):
                    edge_iteration(l, GROUPS - RING + r, r)
                edge_sum(l, GROUPS - 1, RING - 1)

                turn(l, 1, 0)
                for c in range(NCH):
                    if c + 1 < NCH:
                        turn(l, 1, c + 1)
                    attention_out(l, c)
                turn(l, 2, 0, n=2 * l + 2)
                for c in range(NCH):
                    if c + 1 < NCH:
                        turn(l, 2, c + 1, n=2 * l + 2)
                    hidden(l, c)
                    if c >= 1:
                        ff_out(l, c - 1)
                ff_out(l, NCH - 1)

        @program.scalar
        def _(act):
            def root_var(n):
                act.wait_ge(s_var, (n + 1) * BLOCKS)
                act.activation(std[:], mv[:, :, 1], ACT.Sqrt, bias=eps[:]).then_inc(s_std, 1)

            act.wait_ge(s_const, CONSTS)
            act.wait_ge(s_degsum_ps, 1)
            act.activation(degstd[:], bank[0][:, 0:1], ACT.Sqrt, scale=1.0 / (N - 1)).then_inc(s_degstd, 1)
            root_var(0)

            def untranspose(l, phase, c, gain=None, shift=None):
                t = tp_no(l, phase, c)
                act.wait_ge(s_tp, t + 1)
                source = bank[t % 2][:, 0:CHUNKS[c][1] * P]
                if gain is None:
                    act.copy(xnT[:, chunk_cols(c)], source).then_inc(s_xnT, 1)
                else:
                    act.activation(xnT[:, chunk_cols(c)], source, ACT.Identity, bias=w[l][:, shift:shift + 1], scale=w[l][:, gain:gain + 1]).then_inc(s_xnT, 1)

            def q_first(l, c):
                act.wait_ge(s_qkv, l * BLOCKS + CHUNKS[c][0] + CHUNKS[c][1])
                act.copy(chunk_blocks(qp[:, :, 0, :], c), chunk_blocks(qkv[:, :, 0:D], c)).then_inc(s_q1, 1)

            def q_second(l, c):
                act.wait_ge(s_r1, l * NCH + c + 1)
                act.copy(chunk_blocks(qp[:, :, 1, :], c), qres[:, c % 2, 0:CHUNKS[c][1], :]).then_inc(s_q2, 1)

            def edge_copy(l, g, r):
                n = l * GROUPS + g
                act.wait_ge(s_ohT_ps, n + 1)
                act.copy(onehotT[:, r % 2, :, :].rearrange("p j e -> p (j e)"), bank[r % 2][:].bitcast(BF16)[:, 0:G * P]).then_inc(s_ohT, 1)

            def edge_exp(l, g, r):
                n = l * GROUPS + g
                act.wait_ge(s_attc, n + 1)
                act.activation(msg[:, r % 2, :, D:AGG], attc[:, r % 2, :].rearrange("p (j h) -> p j h", h=H), ACT.Exp).then_inc(s_ex, 1)

            def edge_iteration(l, g, r):
                edge_exp(l, g, r)
                if given(g, 0, GROUPS - 2):
                    edge_copy(l, g + 2, (r + 2) % RING)

            def gelu(l, c):
                for f in range(FC):
                    act.wait_ge(s_ff1, (l * NCH + c) * FC + f + 1)
                    if c >= 2:
                        act.wait_ge(s_y_ps, l * NCH + c - 1)
                    n = CHUNKS[c][1] * P
                    act.activation(hT[:, c % 2, f, 0:n], bank[4 + f][:, 0:n], ACT.Gelu, bias=w[l][:, V_FF + f:V_FF + f + 1]).then_inc(s_gelu, 1)

            act.wait_ge(s_w, 16 * (2 * L + 1))
            for l in range(L):
                root_var(2 * l + 1)
                untranspose(l, 0, 0, V_G1, V_B1)
                for c in range(NCH + 2):
                    if c + 1 < NCH:
                        untranspose(l, 0, c + 1, V_G1, V_B1)
                    if 0 <= c - 1 < NCH:
                        q_first(l, c - 1)
                    if 0 <= c - 2:
                        q_second(l, c - 2)
                act.wait_ge(s_loop_att, l + 1)
                act.activation(agg[:, :, D:AGG], loop_att[:].rearrange("p (b h) -> p b h", h=H), ACT.Exp).then_inc(s_loop_ex, 1)

                edge_copy(l, 0, 0)
                edge_copy(l, 1, 1)
                for g in range(RING):
                    edge_iteration(l, g, g)
                with act.Fori(1, ROUNDS - 1) as it:
                    for r in range(RING):
                        edge_iteration(l, it * RING + r, r)
                for r in range(RING):
                    edge_iteration(l, GROUPS - RING + r, r)

                for c in range(NCH):
                    untranspose(l, 1, c)
                root_var(2 * l + 2)
                untranspose(l, 2, 0, V_G2, V_B2)
                for c in range(NCH):
                    if c + 1 < NCH:
                        untranspose(l, 2, c + 1, V_G2, V_B2)
                    gelu(l, c)

        @program.vector
        def _(dve):
            links = [0]

            def link(instruction):
                links[0] += 1
                instruction.then_inc(s_chain, 1)
                dve.wait_ge(s_chain, links[0])

            dve.wait_ge(s_last, 16)
            link(dve.tensor_copy(last_f[:], last_i[:]))
            dve.wait_ge(s_const, CONSTS)
            link(dve.tensor_tensor(before[:], last_f[:].unsqueeze(1).broadcast_to([P, BLOCKS - 1, TC]), thr[:].unsqueeze(2).broadcast_to([P, BLOCKS - 1, TC]), ALU.is_lt))
            dve.tensor_reduce(count[:], before[:], AX, ALU.add).then_inc(s_count, 1)
            dve.wait_ge(s_first_ps, 1)
            link(dve.tensor_tensor(first[:], bank[0][:, 0:BLOCKS - 1], blockno[:], ALU.add))
            link(dve.tensor_tensor(begun[:], first[:].unsqueeze(1).broadcast_to([P, SC, BLOCKS - 1]), stepno[:].unsqueeze(2).broadcast_to([P, SC, BLOCKS - 1]), ALU.is_le))
            dve.tensor_reduce(block[:], begun[:], AX, ALU.add).then_inc(s_block, 1)
            dve.wait_ge(s_block, 1)
            link(dve.tensor_tensor(stepno[:], stepno[:], block[:], ALU.subtract))
            dve.tensor_scalar(tileno[:], stepno[:], float(TILES_P - 1), None, ALU.min).then_inc(s_tileno, 1)
            link(dve.tensor_scalar(block128[:], block[:], float(P), None, ALU.mult))
            dve.wait_ge(s_blockT_ps, 1)
            dve.tensor_copy(blockT[:], bank[1][0:SC, 0:P]).then_inc(s_blockT, 1)

            dve.wait_ge(s_src, 16)
            link(dve.tensor_scalar(part_i, src_nat, P - 1, None, ALU.bitwise_and))
            link(dve.tensor_copy(lo, part_i))
            link(dve.tensor_scalar(part_i, src_nat, 7, None, ALU.logical_shift_right))
            dve.tensor_copy(hi, part_i).then_inc(s_digits, 1)
            dve.wait_ge(s_digits, 1)

            def hist_step(k, buf, t0):
                if not isinstance(k, int) or k >= 2:
                    dve.wait_ge(s_hist_mm, k - 1)
                dve.tensor_tensor(oh_hi[:, buf, :, :], iota_bf[:, 0:BLOCKS].unsqueeze(1).broadcast_to([P, HT, BLOCKS]),
                                  hi[:, bass.ds(t0, HT)].unsqueeze(2).broadcast_to([P, HT, BLOCKS]), ALU.is_equal)
                for j in range(HT):
                    ins = dve.tensor_scalar(oh_lo[:, buf, j, :], iota_bf[:], lo[:, bass.ds(t0 + j, 1)], None, ALU.is_equal)
                ins.then_inc(s_hist_oh, 1)

            hist_step(0, 0, 0)
            hist_step(1, 1, HT)
            with dve.Fori(1, HSTEPS // 2) as i:
                hist_step(2 * i, 0, 2 * i * HT)
                hist_step(2 * i + 1, 1, (2 * i + 1) * HT)
            if HSTEPS % 2:
                hist_step(HSTEPS - 1, 0, (HSTEPS - 1) * HT)
            dve.wait_ge(s_hist_mm, HSTEPS)
            link(dve.tensor_scalar(deg[:], bank[2][:, 0:BLOCKS], 1.0 - (E + N) / N, None, ALU.add))
            link(dve.tensor_tensor(deg[:], deg[:], valid[:], ALU.mult))
            link(dve.tensor_tensor(degsq[:], deg[:], deg[:], ALU.mult))
            dve.tensor_reduce(degsum[:], degsq[:], AX, ALU.add).then_inc(s_degsum, 1)
            dve.wait_ge(s_degstd, 1)
            link(dve.tensor_scalar(degstd[:], degstd[:], 1e-6, None, ALU.add))
            link(dve.reciprocal(degstd[:], degstd[:]))
            dve.tensor_scalar(deg[:], deg[:], degstd[:], None, ALU.mult).then_inc(s_deg, 1)
            dve.wait_ge(s_degT_ps, 1)
            dve.tensor_copy(degT[:], bank[1][0:BLOCKS, 0:P]).then_inc(s_degT, 1)

            dve.wait_ge(s_rows, 16 * 2 * SC)
            for c in range(SC):
                dve.tensor_scalar(step_dst_f[:, c * P:(c + 1) * P], step_dst[:, c * P:(c + 1) * P], block128[:, c:c + 1], None, ALU.subtract).then_inc(s_rows_f, 1)
            for c in range(SC):
                dve.tensor_copy(step_src_f[:, c * P:(c + 1) * P], step_src[:, c * P:(c + 1) * P]).then_inc(s_rows_f, 1)
            for k in range(2 * SC):
                dve.wait_ge(s_rowsT_ps, k + 1)
                dve.tensor_copy((rel if k < SC else srcidx)[:, k % SC * P:(k % SC + 1) * P], bank[3 + k % 2][:, 0:P]).then_inc(s_rowsT, 1)
            dve.wait_ge(s_rowsT, 2 * SC)
            link(dve.tensor_copy(rel[:, STEPS_P:STEPS_P + G * RING], rel[:, 0:G * RING]))
            link(dve.tensor_copy(srcidx[:, STEPS_P:STEPS_P + G * RING], srcidx[:, 0:G * RING]))

            def norm_stats(n, c, source):
                b0, nb = CHUNKS[c]
                for b in range(b0, b0 + nb):
                    dve.bn_stats(stats[:, b, :], source[:, b, :]).then_inc(s_stats, 1)
                dve.wait_ge(s_stats, n * BLOCKS + b0 + nb)
                for b in range(b0, b0 + nb):
                    dve.bn_aggr(mv[:, b, :], stats[:, b, :]).then_inc(s_var, 1)

            def normalise(n, target, source):
                dve.wait_ge(s_std, n + 1)
                dve.reciprocal(rstd[:], std[:]).then_inc(s_rstd, 1)
                dve.wait_ge(s_rstd, n + 1)
                for b in range(BLOCKS):
                    dve.tensor_scalar(target[:, b, :], source[:, b, :], mv[:, b, 0:1], rstd[:, b:b + 1], ALU.subtract, ALU.mult).then_inc(s_xn, 1)

            dve.wait_ge(s_x, 16)
            for c in range(NCH):
                norm_stats(0, c, x0)
            normalise(0, x, x0)
            dve.wait_ge(s_xn, BLOCKS)
            link(dve.tensor_scalar(x[:], x[:], 0.0, None, ALU.max))
            for c in range(NCH):
                norm_stats(1, c, x)

            dve.wait_ge(s_w, 16 * (2 * L + 1))
            for l in range(L):
                link(dve.tensor_tensor(pos_bias[:, l:l + 1], w[l][:, V_POS:V_POS + 1], w[l][:, V_DEG:V_DEG + 1], ALU.add))
                link(dve.tensor_scalar(w[l][:, W_QKV:W_QKV + D], w[l][:, W_QKV:W_QKV + D], HD ** -0.5, None, ALU.mult))
                link(dve.tensor_scalar(row[l][:, R_QKV:R_QKV + D], row[l][:, R_QKV:R_QKV + D], HD ** -0.5, None, ALU.mult))

            def position(l, c):
                dve.wait_ge(s_xp_ps, l * NCH + c + 1)
                cols = chunk_cols(c)
                dve.scalar_tensor_tensor(out=xnT[:, cols], in0=bank[2 + c % 2][:, 0:CHUNKS[c][1] * P], scalar=pos_bias[:, l:l + 1],
                                         in1=xnT[:, cols], op0=ALU.add, op1=ALU.add).then_inc(s_xpT, 1)

            def qkv_bias(l, c):
                b0, nb = CHUNKS[c]
                for b in range(b0, b0 + nb):
                    dve.wait_ge(s_qkv_ps, l * BLOCKS + b + 1)
                    dve.tensor_tensor(qkv[:, b, :], bank[4 + b % 4][:, 0:3 * D], row[l][:, R_QKV:R_QKV + 3 * D], ALU.add).then_inc(s_qkv, 1)

            def q_rest(l, c):
                dve.wait_ge(s_q1, l * NCH + c + 1)
                if l or c >= 2:
                    dve.wait_ge(s_q3, l * NCH + c - 1)
                dve.tensor_tensor(qres[:, c % 2, 0:CHUNKS[c][1], :], chunk_blocks(qkv[:, :, 0:D], c), chunk_blocks(qp[:, :, 0, :], c), ALU.subtract).then_inc(s_r1, 1)

            def q_third(l, c):
                dve.wait_ge(s_q2, l * NCH + c + 1)
                dve.tensor_tensor(chunk_blocks(qp[:, :, 2, :], c), qres[:, c % 2, 0:CHUNKS[c][1], :], chunk_blocks(qp[:, :, 1, :], c), ALU.subtract).then_inc(s_q3, 1)

            def by_head(t):
                return t.rearrange("p b (h d) -> p b h d", d=HD)

            def self_loops(l):
                dve.wait_ge(s_qkv, (l + 1) * BLOCKS)
                link(dve.tensor_tensor(xn[:], qkv[:, :, 0:D], qkv[:, :, D:2 * D], ALU.mult))
                link(dve.tensor_reduce(loop_att[:], xn[:].rearrange("p b (h d) -> p (b h) d", d=HD), AX, ALU.add))
                link(dve.tensor_tensor(loop_nan[:], loop_att[:], loop_att[:], ALU.not_equal))
                link(dve.tensor_scalar(loop_att[:], loop_att[:], -50.0, 50.0, ALU.max, ALU.min))
                dve.copy_predicated(loop_att[:], loop_nan[:], zeros[:]).then_inc(s_loop_att, 1)
                dve.tensor_tensor(x[:], x[:], row[l][:, R_O:R_O + D].unsqueeze(1).broadcast_to([P, BLOCKS, D]), ALU.add).then_inc(s_bias, 1)
                dve.wait_ge(s_loop_ex, l + 1)
                dve.tensor_tensor(by_head(agg[:, :, 0:D]), by_head(qkv[:, :, 2 * D:3 * D]),
                                  agg[:, :, D:AGG].unsqueeze(3).broadcast_to([P, BLOCKS, H, HD]), ALU.mult).then_inc(s_agg0, 1)
                dve.wait_ge(s_agg0, l + 1)

            def edge_onehot(l, g, r):
                dve.tensor_tensor(onehot[:, r, :, :], iota_free[:].unsqueeze(1).broadcast_to([P, G, P]),
                                  rel[:, bass.ds(g * G, G)].unsqueeze(2).broadcast_to([P, G, P]), ALU.is_equal).then_inc(s_oh, 1)

            def edge_stage(g, r):
                dve.tensor_copy(idx[:, r, :], srcidx[:, bass.ds(g * G, G)]).then_inc(s_idx[r], 1)

            def edge_prod(l, g, r, kv_round):
                n = l * GROUPS + g
                dve.wait_ge(s_kv[r], 16 * G * kv_round)
                dve.wait_ge(s_qe, n + 1)
                dve.tensor_tensor(prod[:], kvr[:, r, :, 0:D], bank[2 + r % 2][:].rearrange("p (j c) -> p j c", c=D), ALU.mult).then_inc(s_prod, 1)

            def edge_att(l, g, r):
                n = l * GROUPS + g
                dve.wait_ge(s_prod, n + 1)
                dve.tensor_reduce(att[:, r % 2, :], prod[:].rearrange("p j (h d) -> p (j h) d", d=HD), AX, ALU.add).then_inc(s_att, 1)

            def edge_clip(l, g, r):
                n = l * GROUPS + g
                dve.wait_ge(s_att, n + 1)
                dve.tensor_tensor(attnan[:, r % 2, :], att[:, r % 2, :], att[:, r % 2, :], ALU.not_equal)
                dve.tensor_scalar(attc[:, r % 2, :], att[:, r % 2, :], -50.0, 50.0, ALU.max, ALU.min).then_inc(s_clip, 1)

            def edge_guard(l, g, r):
                dve.copy_predicated(attc[:, r % 2, :], attnan[:, r % 2, :], zeros[:, 0:G * H]).then_inc(s_attc, 1)

            def edge_msg(l, g, r):
                n = l * GROUPS + g
                dve.wait_ge(s_ex, n + 1)
                dve.tensor_tensor(by_head(msg[:, r % 2, :, 0:D]), by_head(kvr[:, r, :, D:KV]),
                                  msg[:, r % 2, :, D:AGG].unsqueeze(3).broadcast_to([P, G, H, HD]), ALU.mult).then_inc(s_msg, 1)

            def edge_add(g, r, j, blocks):
                target = agg[:, bass.ds(blocks[j], 1), :].rearrange("p a c -> p (a c)")
                dve.tensor_tensor(target, target, agg_bank(r, j), ALU.add).then_inc(s_agg, 1)

            def edge_iteration(l, g, r, kv_round):
                n = l * GROUPS + g
                back, older = (r - 1) % RING, (r - 2) % RING
                adds = given(g, 2)
                blocks = read_blocks(ENG.DVE, g - 2) if adds else None

                def add(j):
                    if adds:
                        if j == 0:
                            dve.wait_ge(s_agg_ps, n - 1)
                        else:
                            dve.wait_ge(s_agg, (n - 2) * G + j)
                        edge_add(g - 2, older, j, blocks)

                edge_prod(l, g, r, kv_round)
                add(0)
                if given(g, 1):
                    edge_msg(l, g - 1, back)
                add(1)
                edge_att(l, g, r)
                if given(g, 1):
                    dve.wait_ge(s_msg, n)
                    edge_stage(g - 1 + RING, back)
                add(2)
                edge_clip(l, g, r)
                dve.wait_ge(s_clip, n + 1)
                add(3)
                edge_guard(l, g, r)
                if adds:
                    dve.wait_ge(s_agg, (n - 1) * G)
                edge_onehot(l, g + 2, (r + 2) % RING)

            for r in range(RING):
                edge_stage(r, r)
            edge_onehot(0, 0, 0)
            edge_onehot(0, 1, 1)
            for l in range(L):
                normalise(2 * l + 1, xn, x)
                for c in range(NCH + 3):
                    if c < NCH:
                        position(l, c)
                    if 0 <= c - 1 < NCH:
                        qkv_bias(l, c - 1)
                    if 0 <= c - 2 < NCH:
                        q_rest(l, c - 2)
                    if 0 <= c - 3:
                        q_third(l, c - 3)
                self_loops(l)

                for g in range(RING):
                    edge_iteration(l, g, g, l * ROUNDS + 1)
                with dve.Fori(1, ROUNDS - 1) as it:
                    for r in range(RING):
                        edge_iteration(l, it * RING + r, r, it + (l * ROUNDS + 1))
                for r in range(RING):
                    edge_iteration(l, GROUPS - RING + r, r, (l + 1) * ROUNDS)
                edge_msg(l, GROUPS - 1, RING - 1)
                for g in (GROUPS - 2, GROUPS - 1):
                    blocks = read_blocks(ENG.DVE, g)
                    dve.wait_ge(s_agg_ps, l * GROUPS + g + 1)
                    for j in range(G):
                        dve.wait_ge(s_agg, (l * GROUPS + g) * G + j)
                        edge_add(g, g % RING, j, blocks)
                dve.wait_ge(s_msg, (l + 1) * GROUPS)
                edge_stage(GROUPS - 1 + RING, RING - 1)

                dve.wait_ge(s_agg, (l + 1) * STEPS_P)
                dve.reciprocal(rsum[:], agg[:, :, D:AGG]).then_inc(s_rsum, 1)
                dve.wait_ge(s_rsum, l + 1)
                for c, (b0, nb) in enumerate(CHUNKS):
                    dve.tensor_tensor(by_head(chunk_blocks(xn, c)), by_head(chunk_blocks(agg[:, :, 0:D], c)),
                                      rsum[:, b0:b0 + nb, :].unsqueeze(3).broadcast_to([P, nb, H, HD]), ALU.mult).then_inc(s_norm, 1)
                dve.wait_ge(s_bias, 2 * l + 1)
                for c in range(NCH):
                    dve.wait_ge(s_o_ps, l * NCH + c + 1)
                    dve.tensor_tensor(chunk_blocks(x, c), chunk_blocks(x, c), chunk_bank(2 + c % 2, c), ALU.add).then_inc(s_o, 1)
                    dve.wait_ge(s_o, l * NCH + c + 1)
                    norm_stats(2 * l + 2, c, x)
                normalise(2 * l + 2, xn, x)
                dve.wait_ge(s_xn, (2 * l + 3) * BLOCKS)
                dve.tensor_tensor(x[:], x[:], row[l][:, R_2:R_2 + D].unsqueeze(1).broadcast_to([P, BLOCKS, D]), ALU.add).then_inc(s_bias, 1)
                dve.wait_ge(s_bias, 2 * l + 2)
                for c in range(NCH):
                    dve.wait_ge(s_y_ps, l * NCH + c + 1)
                    dve.tensor_tensor(chunk_blocks(x, c), chunk_blocks(x, c), chunk_bank(2 + c % 2, c), ALU.add).then_inc(s_y, 1)
                    dve.wait_ge(s_y, l * NCH + c + 1)
                    if l + 1 < L:
                        norm_stats(2 * l + 3, c, x)
                    else:
                        dve.tensor_tensor(chunk_blocks(x0, c), chunk_blocks(x0, c), chunk_blocks(x, c), ALU.add).then_inc(s_final, 1)


OUT_SHAPE = (N, D)


def kernel(**inputs):
    import concourse.bacc as bacc
    from concourse.bass_utils import run_bass_kernel_spmd

    def get(name):
        return np.asarray(inputs["L0_gnn_" + name])

    x_pad = np.concatenate([np.asarray(inputs["x"]), np.zeros((NP - N, D), np.float32)])
    pad = TILES_P * P - E
    src_tiles = np.concatenate([np.asarray(inputs["src"]), np.full(pad, NP - 1, np.int32)]).reshape(TILES_P, P)
    dst_tiles = np.concatenate([np.asarray(inputs["dst"]), np.full(pad, NP, np.int32)]).reshape(TILES_P, P)
    dst_last = np.full((TC * P,), NP, np.int32)
    dst_last[:TILES_P] = dst_tiles[:, P - 1]
    dst_last = np.ascontiguousarray(dst_last.reshape(TC, P).T)
    weights = np.concatenate(
        [get("Wpos"), get("Wq"), get("Wk"), get("Wv"), get("Wo"), get("W1"),
         get("W2").reshape(L, FC, P, D).transpose(0, 2, 1, 3).reshape(L, P, FC * D)]
        + [get(v)[:, :, None] for v in ("ln1_g", "ln1_b", "ln2_g", "ln2_b", "bpos", "bdeg")]
        + [get("b1").reshape(L, FC, P).transpose(0, 2, 1)], axis=2)
    rows = np.concatenate([get(v) for v in ("bq", "bk", "bv", "bo", "b2")], axis=1)
    wdeg = get("Wdeg").reshape(1, L, D)
    arrays = {"x_in": x_pad, "src_tiles": src_tiles, "dst_tiles": dst_tiles, "dst_last": dst_last,
              "weights": weights, "rows": rows, "wdeg_in": wdeg}
    arrays = {k: np.ascontiguousarray(a) for k, a in arrays.items()}

    nc = bacc.Bacc("TRN2", target_bir_lowering=False, num_devices=1)
    args = {k: nc.dram_tensor(k, a.shape, mybir.dt.from_np(a.dtype), kind="ExternalInput").ap() for k, a in arrays.items()}
    out = nc.dram_tensor("out", OUT_SHAPE, F32, kind="ExternalOutput").ap()
    build(nc, out=out, **args)
    result = run_bass_kernel_spmd(nc, [arrays], core_ids=[0])
    return result.results[0]["out"]
```

```python
from contextlib import ExitStack

import numpy as np

import concourse.bass as bass
from concourse import mybir

F32 = mybir.dt.float32
BF16 = mybir.dt.bfloat16
I32 = mybir.dt.int32
U32 = mybir.dt.uint32
U8 = mybir.dt.uint8
ALU = mybir.AluOpType
ACT = mybir.ActivationFunctionType
AX = mybir.AxisListType.X
ENG = mybir.EngineType

P = 128
N, D, H, L, FF = 3125, 128, 8, 2, 512
HD = D // H
E = 103125
BLOCKS = -(-N // P)
NP = BLOCKS * P
TAIL = N - (BLOCKS - 1) * P
TILES = -(-E // P)
G = 4
RING = 4
STEPS = TILES - 1 + BLOCKS
ROUNDS = -(-STEPS // (G * RING))
GROUPS = ROUNDS * RING
STEPS_P = GROUPS * G
TILES_P = STEPS_P - (BLOCKS - 1)
SC = -(-(STEPS_P + G * RING) // P)
TC = -(-TILES_P // P)
FC = FF // P
STEP_CONSTS = 6
CONSTS = 14
KV = 2 * D
AGG = D + H
CB = 4
CHUNKS = [(c * CB, min(CB, BLOCKS - c * CB)) for c in range(-(-BLOCKS // CB))]
NCH = len(CHUNKS)
LO = 64
HI = NP // LO
HT = 52
HSTEPS = -(-TILES // HT)
HE = HSTEPS * HT
W_POS, W_QKV, W_O, W_1, W_2 = 0, D, 4 * D, 5 * D, 5 * D + FF
W_COLS = W_2 + FC * D
V_G1, V_B1, V_G2, V_B2, V_POS, V_DEG, V_FF = range(W_COLS, W_COLS + 7)
W_ALL = V_FF + FC
R_QKV, R_O, R_2 = 0, 3 * D, 4 * D
R_ALL = 5 * D


def given(g, low, high=GROUPS * L * G):
    return not isinstance(g, int) or low <= g < high


def build(nc, x_in, src_flat, src_tiles, dst_tiles, dst_last, weights, rows, wdeg_in, out):
    with ExitStack() as ctx:
        def sb(name, shape, dt=F32):
            return ctx.enter_context(nc.sbuf_tensor(name, shape, dt))

        def sem(name):
            return ctx.enter_context(nc.semaphore(name))

        bank = [ctx.enter_context(nc.psum_tensor(f"bank{i}", [P, 512], F32)) for i in range(8)]

        kv_table = [nc.dram_tensor(f"kv_table{l}", [NP, KV], F32, kind="Internal").ap() for l in range(L)]

        iota_free = sb("iota_free", [P, P])
        ones = sb("ones", [P, P])
        ident = sb("ident", [P, P])
        ident_bf = sb("ident_bf", [P, P], BF16)
        eps = sb("eps", [P, 1])
        zeros = sb("zeros", [P, BLOCKS * H])
        valid = sb("valid", [LO, HI])
        w = [sb(f"w{l}", [P, W_ALL]) for l in range(L)]
        row = [sb(f"row{l}", [P, R_ALL]) for l in range(L)]
        wdeg = sb("wdeg", [1, L, D])
        pos_bias = sb("pos_bias", [P, L])
        x0 = sb("x0", [P, BLOCKS, D])
        x = sb("x", [P, BLOCKS, D])
        xn = sb("xn", [P, BLOCKS, D])
        xnT = sb("xnT", [P, NP])
        qkv = sb("qkv", [P, BLOCKS, 3 * D])
        qp = sb("qp", [P, BLOCKS, 3, D], BF16)
        qres = sb("qres", [P, 2, CB, D])
        agg = sb("agg", [P, BLOCKS, AGG])
        stats = sb("stats", [P, BLOCKS, 6])
        mv = sb("mv", [P, BLOCKS, 2])
        std = sb("std", [P, BLOCKS])
        rstd = sb("rstd", [P, BLOCKS])
        shift0 = sb("shift0", [P, BLOCKS])
        loop_att = sb("loop_att", [P, BLOCKS * H])
        loop_nan = sb("loop_nan", [P, BLOCKS * H], U8)
        rsum = sb("rsum", [P, BLOCKS, H])
        degrow = sb("degrow", [1, NP])
        rel = sb("rel", [P, SC * P])
        srcidx = sb("srcidx", [P, SC * P], U32)
        blockrow = sb("blockrow", [1, SC * P], I32)
        idx = sb("idx", [P, RING, G], U32)
        kvr = sb("kvr", [P, RING, G, KV])
        onehot = sb("onehot", [P, RING, G, P])
        onehotT = sb("onehotT", [P, 2, G, P], BF16)
        prod = sb("prod", [P, G, D])
        att = sb("att", [P, 2, G * H])
        attc = sb("attc", [P, 2, G * H])
        attnan = sb("attnan", [P, 2, G * H], U8)
        msg = sb("msg", [P, 2, G, AGG])
        last_i = sb("last_i", [P, TC], I32)
        last_f = sb("last_f", [P, TC])
        thr = sb("thr", [P, BLOCKS - 1])
        blockno = sb("blockno", [P, BLOCKS - 1])
        before = sb("before", [P, BLOCKS - 1, TC])
        count = sb("count", [P, BLOCKS - 1])
        first = sb("first", [P, BLOCKS - 1])
        stepno = sb("stepno", [P, SC])
        begun = sb("begun", [P, SC, BLOCKS - 1])
        block = sb("block", [P, SC])
        block128 = sb("block128", [P, SC])
        tileno = sb("tileno", [P, SC], U32)
        blockT = sb("blockT", [SC, P], I32)
        deg = sb("deg", [LO, HI])
        degsq = sb("degsq", [LO, HI])
        degsum = sb("degsum", [LO, 1])
        degstd = sb("degstd", [P, 1])
        degT = sb("degT", [HI, LO])
        hT = qkv[:].rearrange("p b c -> p (b c)")[:, 0:2 * FC * 512].rearrange("p (u f n) -> p u f n", u=2, f=FC)
        spare = qkv[:].rearrange("p b c -> p (b c)")
        src_nat = spare[:, 0:HE].bitcast(I32)
        spare_bf = spare[:, HE:].bitcast(BF16)
        low = spare_bf[:, 0:HE]
        high = spare_bf[:, HE:2 * HE]
        spare_bf = spare_bf[:, 2 * HE:]
        digit = spare_bf[:, 0:LO * HT].rearrange("p (n t) -> p n t", t=HT)
        oh_low = spare_bf[:, LO * HT:3 * LO * HT].rearrange("p (u n t) -> p u n t", u=2, t=HT)
        oh_high = spare_bf[:, 3 * LO * HT:(3 * LO + 2 * HI) * HT].rearrange("p (u n t) -> p u n t", u=2, t=HT)
        spare = agg[:].rearrange("p b c -> p (b c)")
        low_i = spare[:, 0:HE].bitcast(I32)
        high_i = spare[:, HE:2 * HE].bitcast(I32)
        spare = kvr[:].rearrange("p r g c -> p (r g c)")
        step_dst, step_src = (spare[:, k * SC * P:(k + 1) * SC * P].bitcast(I32) for k in range(2))
        step_dst_f, step_src_f = (spare[:, k * SC * P:(k + 1) * SC * P] for k in (2, 3))

        s_x = sem("s_x")
        s_last = sem("s_last")
        s_src = sem("s_src")
        s_w = sem("s_w")
        s_const = sem("s_const")
        s_chain = sem("s_chain")
        s_count = sem("s_count")
        s_first_ps = sem("s_first_ps")
        s_block = sem("s_block")
        s_block128 = sem("s_block128")
        s_blockT_ps = sem("s_blockT_ps")
        s_blockT = sem("s_blockT")
        s_blockrow = sem("s_blockrow")
        s_tileno = sem("s_tileno")
        s_rows = sem("s_rows")
        s_rows_f = sem("s_rows_f")
        s_rowsT_ps = sem("s_rowsT_ps")
        s_rowsT = sem("s_rowsT")
        s_digits_i = sem("s_digits_i")
        s_digits = sem("s_digits")
        s_hist_oh = sem("s_hist_oh")
        s_hist_mm = sem("s_hist_mm")
        s_degsum = sem("s_degsum")
        s_degsum_ps = sem("s_degsum_ps")
        s_degstd = sem("s_degstd")
        s_wdeg = sem("s_wdeg")
        s_deg = sem("s_deg")
        s_degT_ps = sem("s_degT_ps")
        s_degT = sem("s_degT")
        s_degrow = sem("s_degrow")
        s_stats = sem("s_stats")
        s_var = sem("s_var")
        s_std = sem("s_std")
        s_rstd = sem("s_rstd")
        s_shift0 = sem("s_shift0")
        s_relu = sem("s_relu")
        s_xn = sem("s_xn")
        s_tp = sem("s_tp")
        s_xnT = sem("s_xnT")
        s_xp_ps = sem("s_xp_ps")
        s_xpT = sem("s_xpT")
        s_qkv_ps = sem("s_qkv_ps")
        s_qkv = sem("s_qkv")
        s_q1 = sem("s_q1")
        s_r1 = sem("s_r1")
        s_q2 = sem("s_q2")
        s_q3 = sem("s_q3")
        s_table = sem("s_table")
        s_loop_att = sem("s_loop_att")
        s_loop_ex = sem("s_loop_ex")
        s_agg0 = sem("s_agg0")
        s_rsum = sem("s_rsum")
        s_norm = sem("s_norm")
        s_o_ps = sem("s_o_ps")
        s_o = sem("s_o")
        s_ff1 = sem("s_ff1")
        s_gelu = sem("s_gelu")
        s_y_ps = sem("s_y_ps")
        s_y = sem("s_y")
        s_bias = sem("s_bias")
        s_final = sem("s_final")
        s_out = sem("s_out")
        s_idx = [sem(f"s_idx{r}") for r in range(RING)]
        s_kv = [sem(f"s_kv{r}") for r in range(RING)]
        s_seen = sem("s_seen")
        s_oh = sem("s_oh")
        s_ohT_ps = sem("s_ohT_ps")
        s_ohT = sem("s_ohT")
        s_qe = sem("s_qe")
        s_prod = sem("s_prod")
        s_att = sem("s_att")
        s_clip = sem("s_clip")
        s_attc = sem("s_attc")
        s_ex = sem("s_ex")
        s_msg = sem("s_msg")
        s_agg_ps = sem("s_agg_ps")
        s_agg = sem("s_agg")

        def chunk_cols(c):
            b0, nb = CHUNKS[c]
            return slice(b0 * P, (b0 + nb) * P)

        def chunk_bank(i, c):
            return bank[i][:, 0:CHUNKS[c][1] * D].rearrange("p (b c) -> p b c", c=D)

        def chunk_blocks(t, c):
            b0, nb = CHUNKS[c]
            return t[:, b0:b0 + nb, :]

        def tp_no(l, phase, c):
            return (l * 3 + phase) * NCH + c

        def xn_no(n, c):
            return (n - 1) * BLOCKS + CHUNKS[c][0] + CHUNKS[c][1]

        def agg_bank(r, j):
            return bank[4 + 2 * (r % 2) + j // 2][:, j % 2 * AGG:(j % 2 + 1) * AGG]

        def read_blocks(engine, g):
            return nc.values_load_multi_w_load_instructions(blockrow[0:1, bass.ds(g * G, G)], engines=(engine,), min_val=0, max_val=BLOCKS - 1,
                                                             skip_runtime_bounds_check_because="a count of the blocks after the first")[1]

        program = ctx.enter_context(nc.Block())

        @program.sync
        def _(sp):
            sp.dma_start(last_i[:], dst_last).then_inc(s_last, 16)
            sp.dma_start(src_nat, src_flat).then_inc(s_src, 16)
            sp.dma_start(x0[:], x_in.rearrange("(b p) c -> p b c", p=P)).then_inc(s_x, 16)
            for l in range(L):
                sp.dma_start(w[l][:], weights[l]).then_inc(s_w, 16)
                sp.dma_start(row[l][:], rows[l:l + 1, :].broadcast_to([P, R_ALL])).then_inc(s_w, 16)
            sp.dma_start(wdeg[:], wdeg_in).then_inc(s_w, 16)
            sp.wait_ge(s_blockT, 1)
            sp.dma_start(blockrow[0:1, :].rearrange("a (c i) -> a c i", i=P), blockT[:].rearrange("c (a i) -> c a i", a=1)).then_inc(s_blockrow, 16)
            sp.wait_ge(s_degT, 1)
            sp.dma_start(degrow[0:1, :].rearrange("a (c i) -> a c i", i=LO), degT[:].rearrange("c (a i) -> c a i", a=1)).then_inc(s_degrow, 16)
            for l in range(L):
                table = kv_table[l].rearrange("(b p) c -> p b c", p=P)
                for c, (b0, nb) in enumerate(CHUNKS):
                    sp.wait_ge(s_qkv, l * BLOCKS + b0 + nb)
                    sp.dma_start(table[:, b0:b0 + nb, :], qkv[:, b0:b0 + nb, D:3 * D]).then_inc(s_table, 16)
            for c, (b0, nb) in enumerate(CHUNKS):
                sp.wait_ge(s_final, c + 1)
                if b0 + nb < BLOCKS:
                    sp.dma_start(out[b0 * P:(b0 + nb) * P, :].rearrange("(b p) c -> p b c", p=P), x0[:, b0:b0 + nb, :]).then_inc(s_out, 16)
                else:
                    sp.dma_start(out[b0 * P:N, :], x0[0:TAIL, b0, :]).then_inc(s_out, 16)
            sp.wait_ge(s_out, 16 * NCH)

        @program.gpsimd
        def _(pool):
            def iota(t, pattern, base, per_partition=0):
                pool.iota(t[:], pattern, base=base, channel_multiplier=per_partition, allow_small_or_imprecise_dtypes=True).then_inc(s_const, 1)

            iota(thr, [[P, BLOCKS - 1]], P)
            iota(blockno, [[1, BLOCKS - 1]], 1)
            iota(stepno, [[P, SC]], 0, 1)
            pool.memset(ones[:], 1.0).then_inc(s_const, 1)
            pool.memset(ident[:], 0.0).then_inc(s_const, 1)
            pool.wait_ge(s_const, 5)
            pool.affine_select(out=ident[:], in_=ident[:], compare_op=ALU.not_equal, fill=1.0, base=0, pattern=[[-1, P]], channel_multiplier=1).then_inc(s_const, 1)
            for t, value in ((ident_bf, 0.0), (valid, 1.0), (eps, 1e-5), (zeros, 0.0)):
                pool.memset(t[:], value).then_inc(s_const, 1)
            iota(digit, [[1, LO], [0, HT]], 0)
            iota(iota_free, [[1, P]], 0)
            pool.wait_ge(s_const, 10)
            pool.affine_select(out=ident_bf[:], in_=ident_bf[:], compare_op=ALU.not_equal, fill=1.0, base=0, pattern=[[-1, P]], channel_multiplier=1).then_inc(s_const, 1)
            pool.affine_select(out=valid[:], in_=valid[:], compare_op=ALU.is_ge, fill=0.0, base=N - 1, pattern=[[-LO, HI]], channel_multiplier=-1).then_inc(s_const, 1)
            pool.wait_ge(s_tileno, 1)
            for rows_of, tiles in ((step_dst, dst_tiles), (step_src, src_tiles)):
                for c in range(SC):
                    pool.indirect_dma_start(rows_of[:, c * P:(c + 1) * P], None, tiles, bass.IndirectOffsetOnAxis(ap=tileno[:, c:c + 1], axis=0)).then_inc(s_rows, 16)
            pool.wait_ge(s_rows, 16 * 2 * SC)
            pool.tensor_copy(step_dst_f, step_dst).then_inc(s_rows_f, 1)
            pool.tensor_copy(step_src_f, step_src).then_inc(s_rows_f, 1)
            pool.wait_ge(s_rows_f, 1)
            pool.wait_ge(s_block128, 1)
            by_step = step_dst_f.rearrange("p (c e) -> p c e", e=P)
            pool.tensor_tensor(by_step, by_step, block128[:].unsqueeze(2).broadcast_to([P, SC, P]), ALU.subtract).then_inc(s_rows_f, 1)

            for l in range(L):
                pool.wait_ge(s_table, 16 * NCH * (l + 1))
                with pool.Fori(0, ROUNDS) as it:
                    for r in range(RING):
                        pool.wait_ge(s_idx[r], it + (l * ROUNDS + 1))
                        pool.sem_inc(s_seen, 1)
                        for j in range(G):
                            pool.indirect_dma_start(kvr[:, r, j, :], None, kv_table[l], bass.IndirectOffsetOnAxis(ap=idx[:, r, j:j + 1], axis=0)).then_inc(s_kv[r], 16)

        @program.tensor
        def _(pe):
            pe.wait_ge(s_const, STEP_CONSTS)
            pe.wait_ge(s_count, 1)
            pe.matmul(bank[0][:, 0:BLOCKS - 1], ones[:], count[:], start=True, stop=True).then_inc(s_first_ps, 1)
            pe.wait_ge(s_block, 1)
            pe.transpose(bank[1][0:SC, 0:P], block[:], ident[:]).then_inc(s_blockT_ps, 1)
            pe.wait_ge(s_const, CONSTS)

            def hist_step(k, buf, start=False, stop=False):
                pe.wait_ge(s_hist_oh, k + 1)
                for t in range(HT):
                    mm = pe.matmul(bank[2][0:LO, 0:HI], oh_low[:, buf, :, t], oh_high[:, buf, :, t], start=start and t == 0, stop=stop and t == HT - 1)
                mm.then_inc(s_hist_mm, 1)

            hist_step(0, 0, start=True)
            with pe.Fori(0, HSTEPS // 2 - 1) as i:
                hist_step(2 * i + 1, 1)
                hist_step(2 * i + 2, 0)
            for k in range(2 * (HSTEPS // 2) - 1, HSTEPS):
                hist_step(k, k % 2, stop=k == HSTEPS - 1)

            pe.wait_ge(s_deg, 1)
            pe.transpose(bank[4][0:HI, 0:LO], deg[:], ident[0:LO, 0:LO]).then_inc(s_degT_ps, 1)
            pe.wait_ge(s_degsum, 1)
            pe.matmul(bank[5][:, 0:1], ones[0:LO, :], degsum[:], start=True, stop=True).then_inc(s_degsum_ps, 1)

            def turn_rows(which, k):
                pe.wait_ge(s_rows_f, 3)
                if which:
                    pe.wait_ge(s_rowsT, k + 1)
                rows_f = (step_dst_f, step_src_f)[which]
                for c in range(k * CB, min(SC, (k + 1) * CB)):
                    mm = pe.transpose(bank[6 + k][:, c % CB * P:(c % CB + 1) * P], rows_f[:, c * P:(c + 1) * P], ident[:])
                mm.then_inc(s_rowsT_ps, 1)

            def turn(l, phase, c, n=None):
                if n is None:
                    pe.wait_ge(s_norm, l * NCH + c + 1)
                else:
                    pe.wait_ge(s_xn, xn_no(n, c))
                t = tp_no(l, phase, c)
                if t >= 2:
                    pe.wait_ge(s_xnT, t - 1)
                b0, nb = CHUNKS[c]
                for b in range(nb):
                    mm = pe.transpose(bank[t % 2][:, b * P:(b + 1) * P], xn[:, b0 + b, :], ident[:])
                mm.then_inc(s_tp, 1)

            def pos(l, c):
                pe.wait_ge(s_xnT, tp_no(l, 0, c) + 1)
                if c >= 2:
                    pe.wait_ge(s_xpT, l * NCH + c - 1)
                o = bank[2 + c % 2][:, 0:CHUNKS[c][1] * P]
                pe.matmul(o, w[l][:, W_POS:W_POS + D], xnT[:, chunk_cols(c)], start=True, stop=False)
                pe.matmul(o, wdeg[0:1, l, :], degrow[0:1, chunk_cols(c)], start=False, stop=True).then_inc(s_xp_ps, 1)

            def project(l, c):
                pe.wait_ge(s_xpT, l * NCH + c + 1)
                b0, nb = CHUNKS[c]
                for b in range(b0, b0 + nb):
                    if b >= 4:
                        pe.wait_ge(s_qkv, l * BLOCKS + b - 3)
                    pe.matmul(bank[4 + b % 4][:, 0:3 * D], xnT[:, b * P:(b + 1) * P], w[l][:, W_QKV:W_QKV + 3 * D], start=True, stop=True).then_inc(s_qkv_ps, 1)

            def edge_turn(l, g, r):
                n = l * GROUPS + g
                pe.wait_ge(s_oh, n + 1)
                view = onehot[:, r, :, :].bitcast(BF16).rearrange("p j (n two) -> p j n two", two=2)
                for j in range(G):
                    mm = pe.transpose(bank[r % 2][:].bitcast(BF16)[:, j * P:(j + 1) * P], view[:, j, :, 1], ident_bf[:])
                mm.then_inc(s_ohT_ps, 1)

            def edge_q(l, g, r, blocks):
                n = l * GROUPS + g
                pe.wait_ge(s_ohT, n + 1)
                for j in range(G):
                    for part in range(3):
                        mm = pe.matmul(bank[2 + r % 2][:, j * D:(j + 1) * D], onehotT[:, r % 2, j, :],
                                       qp[:, bass.ds(blocks[j], 1), part, :].rearrange("p a c -> p (a c)"), start=part == 0, stop=part == 2)
                mm.then_inc(s_qe, 1)

            def edge_sum(l, g, r):
                n = l * GROUPS + g
                pe.wait_ge(s_msg, n + 1)
                for j in range(G):
                    mm = pe.matmul(agg_bank(r, j), onehot[:, r, j, :], msg[:, r % 2, j, :], start=True, stop=True)
                mm.then_inc(s_agg_ps, 1)

            def edge_iteration(l, g, r):
                if given(g, 0, GROUPS - 1):
                    edge_q(l, g + 1, (r + 1) % RING, read_blocks(ENG.PE, g + 1))
                if given(g, 1):
                    edge_sum(l, g - 1, (r - 1) % RING)
                if given(g, 0, GROUPS - 2):
                    edge_turn(l, g + 2, (r + 2) % RING)

            def attention_out(l, c):
                pe.wait_ge(s_xnT, tp_no(l, 1, c) + 1)
                if c >= 2:
                    pe.wait_ge(s_o, l * NCH + c - 1)
                b0, nb = CHUNKS[c]
                for b in range(nb):
                    mm = pe.matmul(bank[2 + c % 2][:, b * D:(b + 1) * D], xnT[:, (b0 + b) * P:(b0 + b + 1) * P], w[l][:, W_O:W_O + D], start=True, stop=True)
                mm.then_inc(s_o_ps, 1)

            def hidden(l, c):
                pe.wait_ge(s_xnT, tp_no(l, 2, c) + 1)
                for f in range(FC):
                    if c >= 1:
                        pe.wait_ge(s_gelu, (l * NCH + c - 1) * FC + f + 1)
                    pe.matmul(bank[4 + f][:, 0:CHUNKS[c][1] * P], w[l][:, W_1 + f * P:W_1 + (f + 1) * P], xnT[:, chunk_cols(c)], start=True, stop=True).then_inc(s_ff1, 1)

            def ff_out(l, c):
                pe.wait_ge(s_gelu, (l * NCH + c + 1) * FC)
                if c >= 2:
                    pe.wait_ge(s_y, l * NCH + c - 1)
                for b in range(CHUNKS[c][1]):
                    for f in range(FC):
                        mm = pe.matmul(bank[2 + c % 2][:, b * D:(b + 1) * D], hT[:, c % 2, f, b * P:(b + 1) * P], w[l][:, W_2 + f * D:W_2 + (f + 1) * D], start=f == 0, stop=f == FC - 1)
                mm.then_inc(s_y_ps, 1)

            pe.wait_ge(s_w, 16 * (2 * L + 1))
            for which in range(2):
                for k in range(2):
                    turn_rows(which, k)
            for l in range(L):
                turn(l, 0, 0, n=2 * l + 1)
                if l == 0:
                    turn(l, 0, 1, n=1)
                    pe.wait_ge(s_degrow, 16)
                    pe.wait_ge(s_wdeg, 1)
                    pe.wait_ge(s_rowsT, 4)
                    pe.wait_ge(s_blockrow, 16)
                for c in range(NCH):
                    if c + 1 < NCH and (l or c):
                        turn(l, 0, c + 1, n=2 * l + 1)
                    pos(l, c)
                    if c >= 1:
                        project(l, c - 1)
                project(l, NCH - 1)

                pe.wait_ge(s_q3, (l + 1) * NCH)
                edge_turn(l, 0, 0)
                edge_turn(l, 1, 1)
                edge_q(l, 0, 0, read_blocks(ENG.PE, 0))
                for g in range(RING):
                    edge_iteration(l, g, g)
                with pe.Fori(1, ROUNDS - 1) as it:
                    for r in range(RING):
                        edge_iteration(l, it * RING + r, r)
                for r in range(RING):
                    edge_iteration(l, GROUPS - RING + r, r)
                edge_sum(l, GROUPS - 1, RING - 1)

                turn(l, 1, 0)
                for c in range(NCH):
                    if c + 1 < NCH:
                        turn(l, 1, c + 1)
                    attention_out(l, c)
                turn(l, 2, 0, n=2 * l + 2)
                for c in range(NCH):
                    if c + 1 < NCH:
                        turn(l, 2, c + 1, n=2 * l + 2)
                    hidden(l, c)
                    if c >= 1:
                        ff_out(l, c - 1)
                ff_out(l, NCH - 1)

        @program.scalar
        def _(act):
            def root_var(n):
                act.wait_ge(s_var, (n + 1) * BLOCKS)
                act.activation(std[:], mv[:, :, 1], ACT.Sqrt, bias=eps[:]).then_inc(s_std, 1)

            act.wait_ge(s_digits_i, 1)
            act.copy(low, low_i).then_inc(s_digits, 1)
            act.wait_ge(s_digits_i, 2)
            act.copy(high, high_i).then_inc(s_digits, 1)
            act.wait_ge(s_const, CONSTS)
            root_var(0)
            act.wait_ge(s_shift0, 1)
            for b in range(BLOCKS):
                act.activation(x[:, b, :], x0[:, b, :], ACT.Relu, bias=shift0[:, b:b + 1], scale=rstd[:, b:b + 1]).then_inc(s_relu, 1)
            root_var(1)
            act.wait_ge(s_degsum_ps, 1)
            act.activation(degstd[:], bank[5][:, 0:1], ACT.Sqrt, scale=1.0 / (N - 1)).then_inc(s_degstd, 1)
            for which, table in enumerate((rel, srcidx)):
                for k in range(2):
                    act.wait_ge(s_rowsT_ps, 2 * which + k + 1)
                    cols = slice(k * CB * P, min(SC, (k + 1) * CB) * P)
                    act.copy(table[:, cols], bank[6 + k][:, 0:cols.stop - cols.start]).then_inc(s_rowsT, 1)
            act.wait_ge(s_rowsT, 4)
            act.copy(rel[:, STEPS_P:STEPS_P + G * RING], rel[:, 0:G * RING]).then_inc(s_rowsT, 1)
            act.copy(srcidx[:, STEPS_P:STEPS_P + G * RING], srcidx[:, 0:G * RING]).then_inc(s_rowsT, 1)

            def untranspose(l, phase, c, gain=None, shift=None):
                t = tp_no(l, phase, c)
                act.wait_ge(s_tp, t + 1)
                source = bank[t % 2][:, 0:CHUNKS[c][1] * P]
                if gain is None:
                    act.copy(xnT[:, chunk_cols(c)], source).then_inc(s_xnT, 1)
                else:
                    act.activation(xnT[:, chunk_cols(c)], source, ACT.Identity, bias=w[l][:, shift:shift + 1], scale=w[l][:, gain:gain + 1]).then_inc(s_xnT, 1)

            def q_first(l, c):
                act.wait_ge(s_qkv, l * BLOCKS + CHUNKS[c][0] + CHUNKS[c][1])
                act.copy(chunk_blocks(qp[:, :, 0, :], c), chunk_blocks(qkv[:, :, 0:D], c)).then_inc(s_q1, 1)

            def q_second(l, c):
                act.wait_ge(s_r1, l * NCH + c + 1)
                act.copy(chunk_blocks(qp[:, :, 1, :], c), qres[:, c % 2, 0:CHUNKS[c][1], :]).then_inc(s_q2, 1)

            def edge_copy(l, g, r):
                n = l * GROUPS + g
                act.wait_ge(s_ohT_ps, n + 1)
                act.copy(onehotT[:, r % 2, :, :].rearrange("p j e -> p (j e)"), bank[r % 2][:].bitcast(BF16)[:, 0:G * P]).then_inc(s_ohT, 1)

            def edge_exp(l, g, r):
                n = l * GROUPS + g
                act.wait_ge(s_attc, n + 1)
                act.activation(msg[:, r % 2, :, D:AGG], attc[:, r % 2, :].rearrange("p (j h) -> p j h", h=H), ACT.Exp).then_inc(s_ex, 1)

            def edge_iteration(l, g, r):
                edge_exp(l, g, r)
                if given(g, 0, GROUPS - 2):
                    edge_copy(l, g + 2, (r + 2) % RING)

            def gelu(l, c):
                for f in range(FC):
                    act.wait_ge(s_ff1, (l * NCH + c) * FC + f + 1)
                    if c >= 2:
                        act.wait_ge(s_y_ps, l * NCH + c - 1)
                    n = CHUNKS[c][1] * P
                    act.activation(hT[:, c % 2, f, 0:n], bank[4 + f][:, 0:n], ACT.Gelu, bias=w[l][:, V_FF + f:V_FF + f + 1]).then_inc(s_gelu, 1)

            act.wait_ge(s_w, 16 * (2 * L + 1))
            for l in range(L):
                if l:
                    root_var(2 * l + 1)
                untranspose(l, 0, 0, V_G1, V_B1)
                for c in range(NCH + 2):
                    if c + 1 < NCH:
                        untranspose(l, 0, c + 1, V_G1, V_B1)
                    if 0 <= c - 1 < NCH:
                        q_first(l, c - 1)
                    if 0 <= c - 2:
                        q_second(l, c - 2)
                act.wait_ge(s_loop_att, l + 1)
                act.activation(agg[:, :, D:AGG], loop_att[:].rearrange("p (b h) -> p b h", h=H), ACT.Exp).then_inc(s_loop_ex, 1)

                edge_copy(l, 0, 0)
                edge_copy(l, 1, 1)
                for g in range(RING):
                    edge_iteration(l, g, g)
                with act.Fori(1, ROUNDS - 1) as it:
                    for r in range(RING):
                        edge_iteration(l, it * RING + r, r)
                for r in range(RING):
                    edge_iteration(l, GROUPS - RING + r, r)

                for c in range(NCH):
                    untranspose(l, 1, c)
                root_var(2 * l + 2)
                untranspose(l, 2, 0, V_G2, V_B2)
                for c in range(NCH):
                    if c + 1 < NCH:
                        untranspose(l, 2, c + 1, V_G2, V_B2)
                    gelu(l, c)

        @program.vector
        def _(dve):
            links = [0]

            def link(instruction):
                links[0] += 1
                instruction.then_inc(s_chain, 1)
                dve.wait_ge(s_chain, links[0])

            dve.wait_ge(s_last, 16)
            link(dve.tensor_copy(last_f[:], last_i[:]))
            dve.wait_ge(s_const, STEP_CONSTS)
            link(dve.tensor_tensor(before[:], last_f[:].unsqueeze(1).broadcast_to([P, BLOCKS - 1, TC]), thr[:].unsqueeze(2).broadcast_to([P, BLOCKS - 1, TC]), ALU.is_lt))
            dve.tensor_reduce(count[:], before[:], AX, ALU.add).then_inc(s_count, 1)
            dve.wait_ge(s_first_ps, 1)
            link(dve.tensor_tensor(first[:], bank[0][:, 0:BLOCKS - 1], blockno[:], ALU.add))
            link(dve.tensor_tensor(begun[:], first[:].unsqueeze(1).broadcast_to([P, SC, BLOCKS - 1]), stepno[:].unsqueeze(2).broadcast_to([P, SC, BLOCKS - 1]), ALU.is_le))
            dve.tensor_reduce(block[:], begun[:], AX, ALU.add).then_inc(s_block, 1)
            dve.wait_ge(s_block, 1)
            link(dve.tensor_tensor(stepno[:], stepno[:], block[:], ALU.subtract))
            dve.tensor_scalar(tileno[:], stepno[:], float(TILES_P - 1), None, ALU.min).then_inc(s_tileno, 1)
            dve.tensor_scalar(block128[:], block[:], float(P), None, ALU.mult).then_inc(s_block128, 1)
            dve.wait_ge(s_blockT_ps, 1)
            dve.tensor_copy(blockT[:], bank[1][0:SC, 0:P]).then_inc(s_blockT, 1)

            dve.wait_ge(s_src, 16)
            dve.tensor_scalar(low_i, src_nat, LO - 1, None, ALU.bitwise_and).then_inc(s_digits_i, 1)
            dve.tensor_scalar(high_i, src_nat, LO.bit_length() - 1, None, ALU.logical_shift_right).then_inc(s_digits_i, 1)

            def norm_stats(n, c, source):
                b0, nb = CHUNKS[c]
                for b in range(b0, b0 + nb):
                    dve.bn_stats(stats[:, b, :], source[:, b, :]).then_inc(s_stats, 1)
                dve.wait_ge(s_stats, n * BLOCKS + b0 + nb)
                for b in range(b0, b0 + nb):
                    dve.bn_aggr(mv[:, b, :], stats[:, b, :]).then_inc(s_var, 1)

            def normalise(n, target, source):
                dve.wait_ge(s_std, n + 1)
                dve.reciprocal(rstd[:], std[:]).then_inc(s_rstd, 1)
                dve.wait_ge(s_rstd, n + 1)
                for b in range(BLOCKS):
                    dve.tensor_scalar(target[:, b, :], source[:, b, :], mv[:, b, 0:1], rstd[:, b:b + 1], ALU.subtract, ALU.mult).then_inc(s_xn, 1)

            dve.wait_ge(s_x, 16)
            for c in range(NCH):
                norm_stats(0, c, x0)
            dve.wait_ge(s_std, 1)
            dve.reciprocal(rstd[:], std[:]).then_inc(s_rstd, 1)
            dve.wait_ge(s_rstd, 1)
            dve.scalar_tensor_tensor(out=shift0[:], in0=mv[:, :, 0], scalar=-1.0, in1=rstd[:], op0=ALU.mult, op1=ALU.mult).then_inc(s_shift0, 1)
            for c, (b0, nb) in enumerate(CHUNKS):
                dve.wait_ge(s_relu, b0 + nb)
                norm_stats(1, c, x)
            normalise(1, xn, x)

            def hist_step(k, buf, t0):
                if not isinstance(k, int) or k >= 2:
                    dve.wait_ge(s_hist_mm, k - 1)
                for oh, values, size in ((oh_low, low, LO), (oh_high, high, HI)):
                    ins = dve.tensor_tensor(oh[:, buf, :, :], digit[:, 0:size, :], values[:, bass.ds(t0, HT)].unsqueeze(1).broadcast_to([P, size, HT]), ALU.is_equal)
                ins.then_inc(s_hist_oh, 1)

            dve.wait_ge(s_const, CONSTS)
            dve.wait_ge(s_digits, 2)
            hist_step(0, 0, 0)
            hist_step(1, 1, HT)
            with dve.Fori(1, HSTEPS // 2) as i:
                hist_step(2 * i, 0, 2 * i * HT)
                hist_step(2 * i + 1, 1, (2 * i + 1) * HT)
            if HSTEPS % 2:
                hist_step(HSTEPS - 1, 0, (HSTEPS - 1) * HT)
            dve.wait_ge(s_hist_mm, HSTEPS)
            dve.scalar_tensor_tensor(out=deg[:], in0=bank[2][0:LO, 0:HI], scalar=1.0 - (E + N) / N, in1=valid[:], op0=ALU.add, op1=ALU.mult).then_inc(s_deg, 1)
            dve.wait_ge(s_deg, 1)
            link(dve.tensor_tensor(degsq[:], deg[:], deg[:], ALU.mult))
            dve.tensor_reduce(degsum[:], degsq[:], AX, ALU.add).then_inc(s_degsum, 1)
            dve.wait_ge(s_degT_ps, 1)
            dve.tensor_copy(degT[:], bank[4][0:HI, 0:LO]).then_inc(s_degT, 1)
            dve.wait_ge(s_w, 16 * (2 * L + 1))
            dve.wait_ge(s_degstd, 1)
            link(dve.tensor_scalar(degstd[:], degstd[:], 1e-6, None, ALU.add))
            link(dve.reciprocal(degstd[:], degstd[:]))
            dve.tensor_scalar(wdeg[:], wdeg[:], degstd[0:1, :], None, ALU.mult).then_inc(s_wdeg, 1)

            for l in range(L):
                link(dve.tensor_tensor(pos_bias[:, l:l + 1], w[l][:, V_POS:V_POS + 1], w[l][:, V_DEG:V_DEG + 1], ALU.add))
                link(dve.tensor_scalar(w[l][:, W_QKV:W_QKV + D], w[l][:, W_QKV:W_QKV + D], HD ** -0.5, None, ALU.mult))
                link(dve.tensor_scalar(row[l][:, R_QKV:R_QKV + D], row[l][:, R_QKV:R_QKV + D], HD ** -0.5, None, ALU.mult))

            def position(l, c):
                dve.wait_ge(s_xp_ps, l * NCH + c + 1)
                cols = chunk_cols(c)
                dve.scalar_tensor_tensor(out=xnT[:, cols], in0=bank[2 + c % 2][:, 0:CHUNKS[c][1] * P], scalar=pos_bias[:, l:l + 1],
                                         in1=xnT[:, cols], op0=ALU.add, op1=ALU.add).then_inc(s_xpT, 1)

            def qkv_bias(l, c):
                b0, nb = CHUNKS[c]
                for b in range(b0, b0 + nb):
                    dve.wait_ge(s_qkv_ps, l * BLOCKS + b + 1)
                    dve.tensor_tensor(qkv[:, b, :], bank[4 + b % 4][:, 0:3 * D], row[l][:, R_QKV:R_QKV + 3 * D], ALU.add).then_inc(s_qkv, 1)

            def q_rest(l, c):
                dve.wait_ge(s_q1, l * NCH + c + 1)
                if l or c >= 2:
                    dve.wait_ge(s_q3, l * NCH + c - 1)
                dve.tensor_tensor(qres[:, c % 2, 0:CHUNKS[c][1], :], chunk_blocks(qkv[:, :, 0:D], c), chunk_blocks(qp[:, :, 0, :], c), ALU.subtract).then_inc(s_r1, 1)

            def q_third(l, c):
                dve.wait_ge(s_q2, l * NCH + c + 1)
                dve.tensor_tensor(chunk_blocks(qp[:, :, 2, :], c), qres[:, c % 2, 0:CHUNKS[c][1], :], chunk_blocks(qp[:, :, 1, :], c), ALU.subtract).then_inc(s_q3, 1)

            def by_head(t):
                return t.rearrange("p b (h d) -> p b h d", d=HD)

            def self_loops(l):
                dve.wait_ge(s_qkv, (l + 1) * BLOCKS)
                link(dve.tensor_tensor(xn[:], qkv[:, :, 0:D], qkv[:, :, D:2 * D], ALU.mult))
                link(dve.tensor_reduce(loop_att[:], xn[:].rearrange("p b (h d) -> p (b h) d", d=HD), AX, ALU.add))
                link(dve.tensor_tensor(loop_nan[:], loop_att[:], loop_att[:], ALU.not_equal))
                link(dve.tensor_scalar(loop_att[:], loop_att[:], -50.0, 50.0, ALU.max, ALU.min))
                dve.copy_predicated(loop_att[:], loop_nan[:], zeros[:]).then_inc(s_loop_att, 1)
                dve.tensor_tensor(x[:], x[:], row[l][:, R_O:R_O + D].unsqueeze(1).broadcast_to([P, BLOCKS, D]), ALU.add).then_inc(s_bias, 1)
                dve.wait_ge(s_loop_ex, l + 1)
                dve.tensor_tensor(by_head(agg[:, :, 0:D]), by_head(qkv[:, :, 2 * D:3 * D]),
                                  agg[:, :, D:AGG].unsqueeze(3).broadcast_to([P, BLOCKS, H, HD]), ALU.mult).then_inc(s_agg0, 1)
                dve.wait_ge(s_agg0, l + 1)

            def edge_onehot(l, g, r):
                dve.tensor_tensor(onehot[:, r, :, :], iota_free[:].unsqueeze(1).broadcast_to([P, G, P]),
                                  rel[:, bass.ds(g * G, G)].unsqueeze(2).broadcast_to([P, G, P]), ALU.is_equal).then_inc(s_oh, 1)

            def edge_stage(g, r):
                dve.tensor_copy(idx[:, r, :], srcidx[:, bass.ds(g * G, G)]).then_inc(s_idx[r], 1)

            def edge_prod(l, g, r, kv_round):
                n = l * GROUPS + g
                dve.wait_ge(s_kv[r], 16 * G * kv_round)
                dve.wait_ge(s_qe, n + 1)
                dve.tensor_tensor(prod[:], kvr[:, r, :, 0:D], bank[2 + r % 2][:].rearrange("p (j c) -> p j c", c=D), ALU.mult).then_inc(s_prod, 1)

            def edge_att(l, g, r):
                n = l * GROUPS + g
                dve.wait_ge(s_prod, n + 1)
                dve.tensor_reduce(att[:, r % 2, :], prod[:].rearrange("p j (h d) -> p (j h) d", d=HD), AX, ALU.add).then_inc(s_att, 1)

            def edge_clip(l, g, r):
                n = l * GROUPS + g
                dve.wait_ge(s_att, n + 1)
                dve.tensor_tensor(attnan[:, r % 2, :], att[:, r % 2, :], att[:, r % 2, :], ALU.not_equal)
                dve.tensor_scalar(attc[:, r % 2, :], att[:, r % 2, :], -50.0, 50.0, ALU.max, ALU.min).then_inc(s_clip, 1)

            def edge_guard(l, g, r):
                dve.copy_predicated(attc[:, r % 2, :], attnan[:, r % 2, :], zeros[:, 0:G * H]).then_inc(s_attc, 1)

            def edge_msg(l, g, r):
                n = l * GROUPS + g
                dve.wait_ge(s_ex, n + 1)
                dve.tensor_tensor(by_head(msg[:, r % 2, :, 0:D]), by_head(kvr[:, r, :, D:KV]),
                                  msg[:, r % 2, :, D:AGG].unsqueeze(3).broadcast_to([P, G, H, HD]), ALU.mult).then_inc(s_msg, 1)

            def edge_add(g, r, j, blocks):
                target = agg[:, bass.ds(blocks[j], 1), :].rearrange("p a c -> p (a c)")
                dve.tensor_tensor(target, target, agg_bank(r, j), ALU.add).then_inc(s_agg, 1)

            def edge_iteration(l, g, r, kv_round):
                n = l * GROUPS + g
                back, older = (r - 1) % RING, (r - 2) % RING
                adds = given(g, 2)
                blocks = read_blocks(ENG.DVE, g - 2) if adds else None

                def add(j):
                    if adds:
                        if j == 0:
                            dve.wait_ge(s_agg_ps, n - 1)
                        else:
                            dve.wait_ge(s_agg, (n - 2) * G + j)
                        edge_add(g - 2, older, j, blocks)

                edge_prod(l, g, r, kv_round)
                add(0)
                if given(g, 1):
                    edge_msg(l, g - 1, back)
                add(1)
                edge_att(l, g, r)
                if given(g, 1):
                    dve.wait_ge(s_msg, n)
                    edge_stage(g - 1 + RING, back)
                add(2)
                edge_clip(l, g, r)
                dve.wait_ge(s_clip, n + 1)
                add(3)
                edge_guard(l, g, r)
                if adds:
                    dve.wait_ge(s_agg, (n - 1) * G)
                edge_onehot(l, g + 2, (r + 2) % RING)

            dve.wait_ge(s_rowsT, 6)
            for r in range(RING):
                edge_stage(r, r)
            edge_onehot(0, 0, 0)
            edge_onehot(0, 1, 1)
            for l in range(L):
                if l:
                    normalise(2 * l + 1, xn, x)
                for c in range(NCH + 3):
                    if c < NCH:
                        position(l, c)
                    if 0 <= c - 1 < NCH:
                        qkv_bias(l, c - 1)
                    if 0 <= c - 2 < NCH:
                        q_rest(l, c - 2)
                    if 0 <= c - 3:
                        q_third(l, c - 3)
                self_loops(l)

                for g in range(RING):
                    edge_iteration(l, g, g, l * ROUNDS + 1)
                with dve.Fori(1, ROUNDS - 1) as it:
                    for r in range(RING):
                        edge_iteration(l, it * RING + r, r, it + (l * ROUNDS + 1))
                for r in range(RING):
                    edge_iteration(l, GROUPS - RING + r, r, (l + 1) * ROUNDS)
                edge_msg(l, GROUPS - 1, RING - 1)
                for g in (GROUPS - 2, GROUPS - 1):
                    blocks = read_blocks(ENG.DVE, g)
                    dve.wait_ge(s_agg_ps, l * GROUPS + g + 1)
                    for j in range(G):
                        dve.wait_ge(s_agg, (l * GROUPS + g) * G + j)
                        edge_add(g, g % RING, j, blocks)
                dve.wait_ge(s_msg, (l + 1) * GROUPS)
                edge_stage(GROUPS - 1 + RING, RING - 1)

                dve.wait_ge(s_agg, (l + 1) * STEPS_P)
                dve.reciprocal(rsum[:], agg[:, :, D:AGG]).then_inc(s_rsum, 1)
                dve.wait_ge(s_rsum, l + 1)
                for c, (b0, nb) in enumerate(CHUNKS):
                    dve.tensor_tensor(by_head(chunk_blocks(xn, c)), by_head(chunk_blocks(agg[:, :, 0:D], c)),
                                      rsum[:, b0:b0 + nb, :].unsqueeze(3).broadcast_to([P, nb, H, HD]), ALU.mult).then_inc(s_norm, 1)
                dve.wait_ge(s_bias, 2 * l + 1)
                for c in range(NCH):
                    dve.wait_ge(s_o_ps, l * NCH + c + 1)
                    dve.tensor_tensor(chunk_blocks(x, c), chunk_blocks(x, c), chunk_bank(2 + c % 2, c), ALU.add).then_inc(s_o, 1)
                    dve.wait_ge(s_o, l * NCH + c + 1)
                    norm_stats(2 * l + 2, c, x)
                normalise(2 * l + 2, xn, x)
                dve.wait_ge(s_xn, (2 * l + 2) * BLOCKS)
                dve.tensor_tensor(x[:], x[:], row[l][:, R_2:R_2 + D].unsqueeze(1).broadcast_to([P, BLOCKS, D]), ALU.add).then_inc(s_bias, 1)
                dve.wait_ge(s_bias, 2 * l + 2)
                for c in range(NCH):
                    dve.wait_ge(s_y_ps, l * NCH + c + 1)
                    dve.tensor_tensor(chunk_blocks(x, c), chunk_blocks(x, c), chunk_bank(2 + c % 2, c), ALU.add).then_inc(s_y, 1)
                    dve.wait_ge(s_y, l * NCH + c + 1)
                    if l + 1 < L:
                        norm_stats(2 * l + 3, c, x)
                    else:
                        dve.tensor_tensor(chunk_blocks(x0, c), chunk_blocks(x0, c), chunk_blocks(x, c), ALU.add).then_inc(s_final, 1)


OUT_SHAPE = (N, D)


def kernel(**inputs):
    import concourse.bacc as bacc
    from concourse.bass_utils import run_bass_kernel_spmd

    def get(name):
        return np.asarray(inputs["L0_gnn_" + name])

    x_pad = np.concatenate([np.asarray(inputs["x"]), np.zeros((NP - N, D), np.float32)])
    pad = TILES_P * P - E
    src_tiles = np.concatenate([np.asarray(inputs["src"]), np.full(pad, NP - 1, np.int32)]).reshape(TILES_P, P)
    dst_tiles = np.concatenate([np.asarray(inputs["dst"]), np.full(pad, NP, np.int32)]).reshape(TILES_P, P)
    src_flat = np.concatenate([np.asarray(inputs["src"]), np.full(HE * P - E, NP - 1, np.int32)]).reshape(P, HE)
    dst_last = np.full((TC * P,), NP, np.int32)
    dst_last[:TILES_P] = dst_tiles[:, P - 1]
    dst_last = np.ascontiguousarray(dst_last.reshape(TC, P).T)
    weights = np.concatenate(
        [get("Wpos"), get("Wq"), get("Wk"), get("Wv"), get("Wo"), get("W1"),
         get("W2").reshape(L, FC, P, D).transpose(0, 2, 1, 3).reshape(L, P, FC * D)]
        + [get(v)[:, :, None] for v in ("ln1_g", "ln1_b", "ln2_g", "ln2_b", "bpos", "bdeg")]
        + [get("b1").reshape(L, FC, P).transpose(0, 2, 1)], axis=2)
    rows = np.concatenate([get(v) for v in ("bq", "bk", "bv", "bo", "b2")], axis=1)
    wdeg = get("Wdeg").reshape(1, L, D)
    arrays = {"x_in": x_pad, "src_flat": src_flat, "src_tiles": src_tiles, "dst_tiles": dst_tiles, "dst_last": dst_last,
              "weights": weights, "rows": rows, "wdeg_in": wdeg}
    arrays = {k: np.ascontiguousarray(a) for k, a in arrays.items()}

    nc = bacc.Bacc("TRN2", target_bir_lowering=False, num_devices=1)
    args = {k: nc.dram_tensor(k, a.shape, mybir.dt.from_np(a.dtype), kind="ExternalInput").ap() for k, a in arrays.items()}
    out = nc.dram_tensor("out", OUT_SHAPE, F32, kind="ExternalOutput").ap()
    build(nc, out=out, **args)
    result = run_bass_kernel_spmd(nc, [arrays], core_ids=[0])
    return result.results[0]["out"]
```

```python
from contextlib import ExitStack

import numpy as np

import concourse.bass as bass
from concourse import mybir

F32 = mybir.dt.float32
BF16 = mybir.dt.bfloat16
I32 = mybir.dt.int32
U32 = mybir.dt.uint32
U8 = mybir.dt.uint8
ALU = mybir.AluOpType
ACT = mybir.ActivationFunctionType
AX = mybir.AxisListType.X
ENG = mybir.EngineType

P = 128
N, D, H, L, FF = 3125, 128, 8, 2, 512
HD = D // H
E = 103125
BLOCKS = -(-N // P)
NP = BLOCKS * P
TAIL = N - (BLOCKS - 1) * P
TILES = -(-E // P)
G = 4
RING = 4
STEPS = TILES - 1 + BLOCKS
ROUNDS = -(-STEPS // (G * RING))
GROUPS = ROUNDS * RING
STEPS_P = GROUPS * G
PADS = STEPS_P - STEPS
TILES_P = STEPS_P - (BLOCKS - 1)
SC = -(-(STEPS_P + G * RING) // P)
TC = -(-TILES_P // P)
FC = FF // P
STEP_CONSTS = 6
CONSTS = 15
KV = 2 * D
AGG = D + H
CB = 4
CHUNK_SIZES = (2, 4, 4, 4, 4, 4, 3)
CHUNKS = [(sum(CHUNK_SIZES[:c]), size) for c, size in enumerate(CHUNK_SIZES)]
NCH = len(CHUNKS)
LO = 64
HI = NP // LO
POOL_ROUNDS = 3
LAG_LN2, LAG_W1, LAG_W2, LAG_LN1, LAG_QKV, LAG_Q = 1, 1, 2, 2, 3, 4
HT = 52
HSTEPS = -(-TILES // HT)
HE = HSTEPS * HT
W_POS, W_QKV, W_O, W_1, W_2 = 0, D, 4 * D, 5 * D, 5 * D + FF
W_COLS = W_2 + FC * D
V_G1, V_B1, V_G2, V_B2, V_POS, V_DEG, V_FF = range(W_COLS, W_COLS + 7)
W_ALL = V_FF + FC
R_QKV, R_O, R_2 = 0, 3 * D, 4 * D
R_ALL = 5 * D


def slots(post, pre):
    return range(0 if post is not None else LAG_LN1, NCH + (LAG_Q if pre is not None else LAG_W2))


def turn_numbers():
    numbers = {}
    for phase in range(L + 1):
        post, pre = (phase - 1 if phase else None), (phase if phase < L else None)
        for i in slots(post, pre):
            for l, which, lag in ((post, "out", 0), (post, "ln2", LAG_LN2), (pre, "ln1", LAG_LN1)):
                if l is not None and 0 <= i - lag < NCH:
                    numbers[l, which, i - lag] = len(numbers)
    return numbers


TURN = turn_numbers()


def given(g, low, high=GROUPS * L * G):
    return not isinstance(g, int) or low <= g < high


def build(nc, x_in, src_flat, src_tiles, dst_tiles, dst_last, weights, rows, wdeg_in, out):
    with ExitStack() as ctx:
        def sb(name, shape, dt=F32):
            return ctx.enter_context(nc.sbuf_tensor(name, shape, dt))

        def sem(name):
            return ctx.enter_context(nc.semaphore(name))

        bank = [ctx.enter_context(nc.psum_tensor(f"bank{i}", [P, 512], F32)) for i in range(8)]

        kv_table = [nc.dram_tensor(f"kv_table{l}", [NP, KV], F32, kind="Internal").ap() for l in range(L)]

        iota_free = sb("iota_free", [P, P])
        ones = sb("ones", [P, P])
        ident = sb("ident", [P, P])
        ident_bf = sb("ident_bf", [P, P], BF16)
        eps = sb("eps", [P, 1])
        zeros = sb("zeros", [P, BLOCKS * H])
        valid = sb("valid", [LO, HI])
        w = [sb(f"w{l}", [P, W_ALL]) for l in range(L)]
        row = [sb(f"row{l}", [P, R_ALL]) for l in range(L)]
        wdeg = sb("wdeg", [1, L, D])
        pos_bias = sb("pos_bias", [P, L])
        x0 = sb("x0", [P, BLOCKS, D])
        x = sb("x", [P, BLOCKS, D])
        xn = sb("xn", [P, BLOCKS, D])
        xnT = sb("xnT", [P, NP])
        qkv = sb("qkv", [P, BLOCKS, 3 * D])
        qp = sb("qp", [P, BLOCKS, 3, D], BF16)
        qres = sb("qres", [P, 2, CB, D])
        agg = sb("agg", [P, BLOCKS, AGG])
        stats = sb("stats", [P, BLOCKS, 6])
        mv = sb("mv", [P, BLOCKS, 2])
        std = sb("std", [P, BLOCKS])
        rstd = sb("rstd", [P, BLOCKS])
        shift = sb("shift", [P, BLOCKS])
        var_eps = sb("var_eps", [P, 2, BLOCKS])
        minus_half = sb("minus_half", [P, CB])
        loop_att = sb("loop_att", [P, BLOCKS * H])
        loop_nan = sb("loop_nan", [P, BLOCKS * H], U8)
        rsum = sb("rsum", [P, BLOCKS, H])
        degrow = sb("degrow", [1, NP])
        rel = sb("rel", [P, SC * P])
        srcidx = sb("srcidx", [P, SC * P], U32)
        blockrow = sb("blockrow", [1, SC * P], I32)
        idx = sb("idx", [P, RING, G], U32)
        kvr = sb("kvr", [P, RING, G, KV])
        onehot = sb("onehot", [P, RING, G, P])
        onehotT = sb("onehotT", [P, 2, G, P], BF16)
        prod = sb("prod", [P, G, D])
        att = sb("att", [P, 2, G * H])
        attc = sb("attc", [P, 2, G * H])
        attnan = sb("attnan", [P, 2, G * H], U8)
        msg = sb("msg", [P, 2, G, AGG])
        last_i = sb("last_i", [P, TC], I32)
        last_f = sb("last_f", [P, TC])
        thr = sb("thr", [P, BLOCKS - 1])
        blockno = sb("blockno", [P, BLOCKS - 1])
        before = sb("before", [P, BLOCKS - 1, TC])
        count = sb("count", [P, BLOCKS - 1])
        first = sb("first", [P, BLOCKS - 1])
        stepno = sb("stepno", [P, SC])
        begun = sb("begun", [P, SC, BLOCKS - 1])
        block = sb("block", [P, SC])
        block128 = sb("block128", [P, SC])
        tileno = sb("tileno", [P, SC], U32)
        blockT = sb("blockT", [SC, P], I32)
        deg = sb("deg", [LO, HI])
        degsq = sb("degsq", [LO, HI])
        degsum = sb("degsum", [LO, 1])
        degstd = sb("degstd", [P, 1])
        degT = sb("degT", [HI, LO])
        hT = kvr[:].rearrange("p r g c -> p (r g c)").rearrange("p (u f n) -> p u f n", u=2, f=FC)
        spare = qkv[:].rearrange("p b c -> p (b c)")
        src_nat = spare[:, 0:HE].bitcast(I32)
        spare_bf = spare[:, HE:].bitcast(BF16)
        low = spare_bf[:, 0:HE]
        high = spare_bf[:, HE:2 * HE]
        spare_bf = spare_bf[:, 2 * HE:]
        digit = spare_bf[:, 0:LO * HT].rearrange("p (n t) -> p n t", t=HT)
        oh_low = spare_bf[:, LO * HT:3 * LO * HT].rearrange("p (u n t) -> p u n t", u=2, t=HT)
        oh_high = spare_bf[:, 3 * LO * HT:(3 * LO + 2 * HI) * HT].rearrange("p (u n t) -> p u n t", u=2, t=HT)
        spare = agg[:].rearrange("p b c -> p (b c)")
        low_i = spare[:, 0:HE].bitcast(I32)
        high_i = spare[:, HE:2 * HE].bitcast(I32)
        x_sums = qp[:].rearrange("p b k c -> p (b k c)")[:, 0:4 * BLOCKS].bitcast(F32).rearrange("p (k b) -> p k b", k=2)
        spare = kvr[:].rearrange("p r g c -> p (r g c)")
        step_dst, step_src = (spare[:, k * SC * P:(k + 1) * SC * P].bitcast(I32) for k in range(2))
        step_dst_f, step_src_f = (spare[:, k * SC * P:(k + 1) * SC * P] for k in (2, 3))

        s_x = sem("s_x")
        s_last = sem("s_last")
        s_src = sem("s_src")
        s_w = sem("s_w")
        s_const = sem("s_const")
        s_chain = sem("s_chain")
        s_count = sem("s_count")
        s_first_ps = sem("s_first_ps")
        s_block = sem("s_block")
        s_block128 = sem("s_block128")
        s_blockT_ps = sem("s_blockT_ps")
        s_blockT = sem("s_blockT")
        s_blockrow = sem("s_blockrow")
        s_tileno = sem("s_tileno")
        s_rows = sem("s_rows")
        s_rows_f = sem("s_rows_f")
        s_rowsT_ps = sem("s_rowsT_ps")
        s_rowsT = sem("s_rowsT")
        s_digits_i = sem("s_digits_i")
        s_digits = sem("s_digits")
        s_hist_oh = sem("s_hist_oh")
        s_hist_mm = sem("s_hist_mm")
        s_degsum = sem("s_degsum")
        s_degsum_ps = sem("s_degsum_ps")
        s_degstd = sem("s_degstd")
        s_wdeg = sem("s_wdeg")
        s_deg = sem("s_deg")
        s_degT_ps = sem("s_degT_ps")
        s_degT = sem("s_degT")
        s_degrow = sem("s_degrow")
        s_squares = sem("s_squares")
        s_stats = sem("s_stats")
        s_sums_in = sem("s_sums_in")
        s_mean_in = sem("s_mean_in")
        s_var_in = sem("s_var_in")
        s_var1 = sem("s_var1")
        s_var2 = sem("s_var2")
        s_std = sem("s_std")
        s_rstd = sem("s_rstd")
        s_shift = sem("s_shift")
        s_var_eps = sem("s_var_eps")
        s_rstd1 = sem("s_rstd1")
        s_rstd2 = sem("s_rstd2")
        s_relu = sem("s_relu")
        s_xn1 = sem("s_xn1")
        s_xn2 = sem("s_xn2")
        s_tp = sem("s_tp")
        s_xnT = sem("s_xnT")
        s_xp_ps = sem("s_xp_ps")
        s_xpT = sem("s_xpT")
        s_qkv_ps = sem("s_qkv_ps")
        s_qkv = sem("s_qkv")
        s_q1 = sem("s_q1")
        s_r1 = sem("s_r1")
        s_q2 = sem("s_q2")
        s_q3 = sem("s_q3")
        s_table = sem("s_table")
        s_loop_att = sem("s_loop_att")
        s_loop_ex = sem("s_loop_ex")
        s_agg0 = sem("s_agg0")
        s_rsum = sem("s_rsum")
        s_norm = sem("s_norm")
        s_o_ps = sem("s_o_ps")
        s_o = sem("s_o")
        s_ff1 = sem("s_ff1")
        s_gelu = sem("s_gelu")
        s_y_ps = sem("s_y_ps")
        s_y = sem("s_y")
        s_bo = sem("s_bo")
        s_b2 = sem("s_b2")
        s_x0 = sem("s_x0")
        s_out = sem("s_out")
        s_idx = [sem(f"s_idx{r}") for r in range(RING)]
        s_kv = [sem(f"s_kv{r}") for r in range(RING)]
        s_seen = sem("s_seen")
        s_oh = sem("s_oh")
        s_ohT_ps = sem("s_ohT_ps")
        s_ohT = sem("s_ohT")
        s_qe = sem("s_qe")
        s_prod = sem("s_prod")
        s_att = sem("s_att")
        s_clip = sem("s_clip")
        s_attc = sem("s_attc")
        s_ex = sem("s_ex")
        s_msg = sem("s_msg")
        s_agg_ps = sem("s_agg_ps")
        s_agg = sem("s_agg")

        def chunk_cols(c):
            b0, nb = CHUNKS[c]
            return slice(b0 * P, (b0 + nb) * P)

        def chunk_bank(i, c):
            return bank[i][:, 0:CHUNKS[c][1] * D].rearrange("p (b c) -> p b c", c=D)

        def chunk_blocks(t, c):
            b0, nb = CHUNKS[c]
            return t[:, b0:b0 + nb, :]

        def blocks_by(c):
            return CHUNKS[c][0] + CHUNKS[c][1]

        def project_bank(l, b):
            return bank[4 + b % 4 if l == 0 else 6 + b % 2]

        def pos_bank(l, c):
            return bank[2 + c % 2 if l == 0 else 4]

        def agg_bank(r, j):
            return bank[4 + 2 * (r % 2) + j // 2][:, j % 2 * AGG:(j % 2 + 1) * AGG]

        def read_blocks(engine, g):
            return nc.values_load_multi_w_load_instructions(blockrow[0:1, bass.ds(g * G, G)], engines=(engine,), min_val=0, max_val=BLOCKS - 1,
                                                             skip_runtime_bounds_check_because="a count of the blocks after the first")[1]

        program = ctx.enter_context(nc.Block())

        @program.sync
        def _(sp):
            sp.dma_start(last_i[:], dst_last).then_inc(s_last, 16)
            sp.dma_start(src_nat, src_flat).then_inc(s_src, 16)
            sp.dma_start(x0[:], x_in.rearrange("(b p) c -> p b c", p=P)).then_inc(s_x, 16)
            for l in range(L):
                sp.dma_start(w[l][:], weights[l]).then_inc(s_w, 16)
                sp.dma_start(row[l][:], rows[l:l + 1, :].broadcast_to([P, R_ALL])).then_inc(s_w, 16)
            sp.dma_start(wdeg[:], wdeg_in).then_inc(s_w, 16)
            sp.wait_ge(s_blockT, 1)
            sp.dma_start(blockrow[0:1, :].rearrange("a (c i) -> a c i", i=P), blockT[:].rearrange("c (a i) -> c a i", a=1)).then_inc(s_blockrow, 16)
            sp.wait_ge(s_degT, 1)
            sp.dma_start(degrow[0:1, :].rearrange("a (c i) -> a c i", i=LO), degT[:].rearrange("c (a i) -> c a i", a=1)).then_inc(s_degrow, 16)
            for l in range(L):
                table = kv_table[l].rearrange("(b p) c -> p b c", p=P)
                for c, (b0, nb) in enumerate(CHUNKS):
                    sp.wait_ge(s_qkv, l * BLOCKS + b0 + nb)
                    sp.dma_start(table[:, b0:b0 + nb, :], qkv[:, b0:b0 + nb, D:3 * D]).then_inc(s_table, 16)
            for c, (b0, nb) in enumerate(CHUNKS):
                sp.wait_ge(s_y, (L - 1) * NCH + c + 1)
                full = min(nb, N // P - b0)
                sp.dma_start(out[b0 * P:(b0 + full) * P, :].rearrange("(b p) c -> p b c", p=P), x[:, b0:b0 + full, :]).then_inc(s_out, 16)
            sp.dma_start(out[N // P * P:N, :], x[0:TAIL, N // P, :]).then_inc(s_out, 16)
            sp.wait_ge(s_out, 16 * (NCH + 1))

        @program.gpsimd
        def _(pool):
            def iota(t, pattern, base, per_partition=0):
                pool.iota(t[:], pattern, base=base, channel_multiplier=per_partition, allow_small_or_imprecise_dtypes=True).then_inc(s_const, 1)

            iota(thr, [[P, BLOCKS - 1]], P)
            iota(blockno, [[1, BLOCKS - 1]], 1)
            iota(stepno, [[P, SC]], 0, 1)
            pool.memset(ones[:], 1.0).then_inc(s_const, 1)
            pool.memset(ident[:], 0.0).then_inc(s_const, 1)
            pool.wait_ge(s_const, 5)
            pool.affine_select(out=ident[:], in_=ident[:], compare_op=ALU.not_equal, fill=1.0, base=0, pattern=[[-1, P]], channel_multiplier=1).then_inc(s_const, 1)
            for t, value in ((ident_bf, 0.0), (valid, 1.0), (eps, 1e-5), (zeros, 0.0), (minus_half, -0.5)):
                pool.memset(t[:], value).then_inc(s_const, 1)
            iota(digit, [[1, LO], [0, HT]], 0)
            iota(iota_free, [[1, P]], 0)
            pool.wait_ge(s_const, 11)
            pool.affine_select(out=ident_bf[:], in_=ident_bf[:], compare_op=ALU.not_equal, fill=1.0, base=0, pattern=[[-1, P]], channel_multiplier=1).then_inc(s_const, 1)
            pool.affine_select(out=valid[:], in_=valid[:], compare_op=ALU.is_ge, fill=0.0, base=N - 1, pattern=[[-LO, HI]], channel_multiplier=-1).then_inc(s_const, 1)
            pool.wait_ge(s_tileno, 1)
            for rows_of, tiles in ((step_dst, dst_tiles), (step_src, src_tiles)):
                for c in range(SC):
                    pool.indirect_dma_start(rows_of[:, c * P:(c + 1) * P], None, tiles, bass.IndirectOffsetOnAxis(ap=tileno[:, c:c + 1], axis=0)).then_inc(s_rows, 16)
            pool.wait_ge(s_rows, 16 * 2 * SC)
            pool.tensor_copy(step_dst_f, step_dst).then_inc(s_rows_f, 1)
            pool.tensor_copy(step_src_f, step_src).then_inc(s_rows_f, 1)
            pool.wait_ge(s_rows_f, 1)
            pool.wait_ge(s_block128, 1)
            by_step = step_dst_f.rearrange("p (c e) -> p c e", e=P)
            pool.tensor_tensor(by_step, by_step, block128[:].unsqueeze(2).broadcast_to([P, SC, P]), ALU.subtract).then_inc(s_rows_f, 1)

            def rstd_chunk(norm, c, s_var, var, s_done):
                b0, nb = CHUNKS[c]
                pool.wait_ge(s_var, var)
                pool.tensor_scalar(var_eps[:, norm - 1, b0:b0 + nb], mv[:, b0:b0 + nb, 1], 1e-5, None, ALU.add).then_inc(s_var_eps, 1)
                eps_added[0] += 1
                pool.wait_ge(s_var_eps, eps_added[0])
                pool.tensor_tensor(rstd[:, b0:b0 + nb], var_eps[:, norm - 1, b0:b0 + nb], minus_half[:, 0:nb], ALU.pow).then_inc(s_done, 1)

            def residual(l, c):
                pool.wait_ge(s_xn2, l * BLOCKS + blocks_by(c))
                xc = chunk_blocks(x, c)
                pool.tensor_tensor(xc, xc, row[l][:, R_2:R_2 + D].unsqueeze(1).broadcast_to([P, CHUNKS[c][1], D]), ALU.add).then_inc(s_b2, 1)
                if l == L - 1:
                    pool.wait_ge(s_b2, l * NCH + c + 1)
                    pool.tensor_tensor(xc, xc, chunk_blocks(x0, c), ALU.add).then_inc(s_x0, 1)

            def gather_round(l, staged, pads=0):
                for r in range(RING):
                    pool.wait_ge(s_idx[r], staged)
                    pool.sem_inc(s_seen, 1)
                    for j in range(G - (pads if r == RING - 1 else 0)):
                        pool.indirect_dma_start(kvr[:, r, j, :], None, kv_table[l], bass.IndirectOffsetOnAxis(ap=idx[:, r, j:j + 1], axis=0)).then_inc(s_kv[r], 16)

            eps_added = [0]
            for l in range(L):
                pool.wait_ge(s_table, 16 * NCH * (l + 1))
                with pool.Fori(0, (ROUNDS - 1) // POOL_ROUNDS) as it:
                    for u in range(POOL_ROUNDS):
                        gather_round(l, it * POOL_ROUNDS + (l * ROUNDS + u + 1))
                gather_round(l, (l + 1) * ROUNDS, pads=PADS)
                pool.wait_ge(s_xn1, (l + 1) * BLOCKS)
                pool.tensor_tensor(x[:], x[:], row[l][:, R_O:R_O + D].unsqueeze(1).broadcast_to([P, BLOCKS, D]), ALU.add).then_inc(s_bo, 1)
                for i in slots(l, l + 1 if l + 1 < L else None):
                    if 0 <= i - LAG_LN2 < NCH:
                        residual(l, i - LAG_LN2)
                    if l + 1 < L and 0 <= i - LAG_LN1 < NCH:
                        rstd_chunk(1, i - LAG_LN1, s_var1, (l + 1) * BLOCKS + blocks_by(i - LAG_LN1), s_rstd1)
                    if i < NCH:
                        rstd_chunk(2, i, s_var2, l * BLOCKS + blocks_by(i), s_rstd2)

        @program.tensor
        def _(pe):
            pe.wait_ge(s_const, STEP_CONSTS)
            pe.wait_ge(s_count, 1)
            pe.matmul(bank[0][:, 0:BLOCKS - 1], ones[:], count[:], start=True, stop=True).then_inc(s_first_ps, 1)
            pe.wait_ge(s_block, 1)
            pe.transpose(bank[1][0:SC, 0:P], block[:], ident[:]).then_inc(s_blockT_ps, 1)
            pe.wait_ge(s_const, CONSTS)

            def hist_step(k, buf, start=False, stop=False):
                pe.wait_ge(s_hist_oh, k + 1)
                for t in range(HT):
                    mm = pe.matmul(bank[2][0:LO, 0:HI], oh_low[:, buf, :, t], oh_high[:, buf, :, t], start=start and t == 0, stop=stop and t == HT - 1)
                mm.then_inc(s_hist_mm, 1)

            def turn_rows(which, k):
                rows_f = (step_dst_f, step_src_f)[which]
                for c in range(k * CB, min(SC, (k + 1) * CB)):
                    mm = pe.transpose(bank[4 + 2 * which + k][:, c % CB * P:(c % CB + 1) * P], rows_f[:, c * P:(c + 1) * P], ident[:])
                mm.then_inc(s_rowsT_ps, 1)

            def hist_pairs(low_pair, high_pair):
                with pe.Fori(low_pair, high_pair) as i:
                    hist_step(2 * i + 1, 1)
                    hist_step(2 * i + 2, 0)

            hist_step(0, 0, start=True)
            hist_pairs(0, HSTEPS // 2 - 3)
            pe.wait_ge(s_rows_f, 3)
            for which in range(2):
                for k in range(2):
                    turn_rows(which, k)
            hist_pairs(HSTEPS // 2 - 3, HSTEPS // 2 - 1)
            for k in range(2 * (HSTEPS // 2) - 1, HSTEPS):
                hist_step(k, k % 2, stop=k == HSTEPS - 1)

            pe.wait_ge(s_deg, 1)
            pe.transpose(bank[2][0:HI, 0:LO], deg[:], ident[0:LO, 0:LO]).then_inc(s_degT_ps, 1)
            pe.wait_ge(s_degsum, 1)
            pe.matmul(bank[3][:, 0:1], ones[0:LO, :], degsum[:], start=True, stop=True).then_inc(s_degsum_ps, 1)

            def turn(l, which, c):
                if which == "out":
                    pe.wait_ge(s_norm, l * NCH + c + 1)
                elif which == "ln1":
                    pe.wait_ge(s_xn1, l * BLOCKS + blocks_by(c))
                else:
                    pe.wait_ge(s_xn2, l * BLOCKS + blocks_by(c))
                t = TURN[l, which, c]
                if t >= 2:
                    pe.wait_ge(s_xnT, t - 1)
                b0, nb = CHUNKS[c]
                for b in range(nb):
                    mm = pe.transpose(bank[t % 2][:, b * P:(b + 1) * P], xn[:, b0 + b, :], ident[:])
                mm.then_inc(s_tp, 1)

            def pos(l, c):
                pe.wait_ge(s_xnT, TURN[l, "ln1", c] + 1)
                if l == 0 and c == 0:
                    pe.wait_ge(s_degrow, 16)
                    pe.wait_ge(s_wdeg, 1)
                banks = 2 if l == 0 else 1
                if c >= banks:
                    pe.wait_ge(s_xpT, l * NCH + c - banks + 1)
                if l >= 1 and c + LAG_LN1 - LAG_W1 < NCH:
                    pe.wait_ge(s_gelu, ((l - 1) * NCH + c + LAG_LN1 - LAG_W1 + 1) * FC - 1)
                o = pos_bank(l, c)[:, 0:CHUNKS[c][1] * P]
                pe.matmul(o, w[l][:, W_POS:W_POS + D], xnT[:, chunk_cols(c)], start=True, stop=False)
                pe.matmul(o, wdeg[0:1, l, :], degrow[0:1, chunk_cols(c)], start=False, stop=True).then_inc(s_xp_ps, 1)

            def project(l, c):
                pe.wait_ge(s_xpT, l * NCH + c + 1)
                b0, nb = CHUNKS[c]
                banks = 4 if l == 0 else 2
                for b in range(b0, b0 + nb):
                    if b >= banks:
                        pe.wait_ge(s_qkv, l * BLOCKS + b - banks + 1)
                    pe.matmul(project_bank(l, b)[:, 0:3 * D], xnT[:, b * P:(b + 1) * P], w[l][:, W_QKV:W_QKV + 3 * D], start=True, stop=True).then_inc(s_qkv_ps, 1)

            def edge_turn(l, g, r):
                n = l * GROUPS + g
                pe.wait_ge(s_oh, n + 1)
                view = onehot[:, r, :, :].bitcast(BF16).rearrange("p j (n two) -> p j n two", two=2)
                for j in range(G):
                    mm = pe.transpose(bank[r % 2][:].bitcast(BF16)[:, j * P:(j + 1) * P], view[:, j, :, 1], ident_bf[:])
                mm.then_inc(s_ohT_ps, 1)

            def edge_q(l, g, r, blocks):
                n = l * GROUPS + g
                pe.wait_ge(s_ohT, n + 1)
                for j in range(G):
                    for part in range(3):
                        mm = pe.matmul(bank[2 + r % 2][:, j * D:(j + 1) * D], onehotT[:, r % 2, j, :],
                                       qp[:, bass.ds(blocks[j], 1), part, :].rearrange("p a c -> p (a c)"), start=part == 0, stop=part == 2)
                mm.then_inc(s_qe, 1)

            def edge_sum(l, g, r):
                n = l * GROUPS + g
                pe.wait_ge(s_msg, n + 1)
                for j in range(G):
                    mm = pe.matmul(agg_bank(r, j), onehot[:, r, j, :], msg[:, r % 2, j, :], start=True, stop=True)
                mm.then_inc(s_agg_ps, 1)

            def edge_iteration(l, g, r):
                if given(g, 0, GROUPS - 1):
                    edge_q(l, g + 1, (r + 1) % RING, read_blocks(ENG.PE, g + 1))
                if given(g, 1):
                    edge_sum(l, g - 1, (r - 1) % RING)
                if given(g, 0, GROUPS - 2):
                    edge_turn(l, g + 2, (r + 2) % RING)

            def attention_out(l, c):
                pe.wait_ge(s_xnT, TURN[l, "out", c] + 1)
                if c >= 1:
                    pe.wait_ge(s_o, l * NCH + c)
                b0, nb = CHUNKS[c]
                for b in range(nb):
                    mm = pe.matmul(bank[2][:, b * D:(b + 1) * D], xnT[:, (b0 + b) * P:(b0 + b + 1) * P], w[l][:, W_O:W_O + D], start=True, stop=True)
                mm.then_inc(s_o_ps, 1)

            def hidden(l, c):
                pe.wait_ge(s_xnT, TURN[l, "ln2", c] + 1)
                for f in range(FC):
                    if c >= 1 or f >= 2:
                        pe.wait_ge(s_gelu, (l * NCH + c) * FC + f - 1)
                    if l + 1 < L and f == 0 and c + LAG_W1 - LAG_LN1 - 1 >= 0:
                        pe.wait_ge(s_xpT, (l + 1) * NCH + c + LAG_W1 - LAG_LN1)
                    pe.matmul(bank[4 + f % 2][:, 0:CHUNKS[c][1] * P], w[l][:, W_1 + f * P:W_1 + (f + 1) * P], xnT[:, chunk_cols(c)], start=True, stop=True).then_inc(s_ff1, 1)

            def ff_out(l, c):
                pe.wait_ge(s_gelu, (l * NCH + c + 1) * FC)
                if c >= 1:
                    pe.wait_ge(s_y, l * NCH + c)
                for b in range(CHUNKS[c][1]):
                    for f in range(FC):
                        mm = pe.matmul(bank[3][:, b * D:(b + 1) * D], hT[:, c % 2, f, b * P:(b + 1) * P], w[l][:, W_2 + f * D:W_2 + (f + 1) * D], start=f == 0, stop=f == FC - 1)
                mm.then_inc(s_y_ps, 1)

            def dense(post, pre):
                if post is None:
                    turn(pre, "ln1", 0)
                    for c in range(NCH + 1):
                        if c + 1 < NCH:
                            turn(pre, "ln1", c + 1)
                        if c < NCH:
                            pos(pre, c)
                        if c >= 1:
                            project(pre, c - 1)
                    return
                for i in slots(post, pre):
                    if post is not None and i < NCH:
                        turn(post, "out", i)
                    if post is not None and 0 <= i - LAG_W2 < NCH:
                        ff_out(post, i - LAG_W2)
                    if post is not None and 0 <= i - LAG_LN2 < NCH:
                        turn(post, "ln2", i - LAG_LN2)
                    if post is not None and i < NCH:
                        attention_out(post, i)
                    if post is not None and 0 <= i - LAG_W1 < NCH:
                        hidden(post, i - LAG_W1)
                    if pre is not None and 0 <= i - LAG_LN1 < NCH:
                        turn(pre, "ln1", i - LAG_LN1)
                    if pre is not None and 0 <= i - LAG_QKV < NCH:
                        project(pre, i - LAG_QKV)
                    if pre is not None and 0 <= i - LAG_LN1 < NCH:
                        pos(pre, i - LAG_LN1)

            pe.wait_ge(s_w, 16 * (2 * L + 1))
            pe.wait_ge(s_rowsT, 4)
            pe.wait_ge(s_blockrow, 16)
            dense(None, 0)
            for l in range(L):
                pe.wait_ge(s_q3, (l + 1) * NCH)
                edge_turn(l, 0, 0)
                edge_turn(l, 1, 1)
                edge_q(l, 0, 0, read_blocks(ENG.PE, 0))
                for g in range(RING):
                    edge_iteration(l, g, g)
                with pe.Fori(1, ROUNDS - 1) as it:
                    for r in range(RING):
                        edge_iteration(l, it * RING + r, r)
                for r in range(RING):
                    edge_iteration(l, GROUPS - RING + r, r)
                edge_sum(l, GROUPS - 1, RING - 1)

                dense(l, l + 1 if l + 1 < L else None)

        @program.scalar
        def _(act):
            def root_var(s_var, count):
                act.wait_ge(s_var, count)
                act.activation(std[:], mv[:, :, 1], ACT.Sqrt, bias=eps[:]).then_inc(s_std, 1)

            act.wait_ge(s_digits_i, 1)
            act.copy(low, low_i).then_inc(s_digits, 1)
            act.wait_ge(s_digits_i, 2)
            act.copy(high, high_i).then_inc(s_digits, 1)
            act.wait_ge(s_const, CONSTS)
            act.wait_ge(s_x, 16)
            for b in range(BLOCKS):
                act.activation(x[:, b, :], x0[:, b, :], ACT.Identity, accum_out=x_sums[:, 0, b:b + 1]).then_inc(s_sums_in, 1)
            act.wait_ge(s_mean_in, 1)
            for b in range(BLOCKS):
                act.activation(x[:, b, :], x0[:, b, :], ACT.Square, bias=shift[:, b:b + 1], accum_out=x_sums[:, 1, b:b + 1]).then_inc(s_sums_in, 1)
            root_var(s_var_in, 1)
            act.wait_ge(s_shift, 1)
            for b in range(BLOCKS):
                act.activation(x[:, b, :], x0[:, b, :], ACT.Relu, bias=shift[:, b:b + 1], scale=rstd[:, b:b + 1], accum_out=x_sums[:, 0, b:b + 1]).then_inc(s_relu, 1)
            act.wait_ge(s_relu, BLOCKS)
            for b in range(BLOCKS):
                act.activation(xn[:, b, :], x[:, b, :], ACT.Square, accum_out=x_sums[:, 1, b:b + 1]).then_inc(s_squares, 1)
            root_var(s_var1, BLOCKS)
            for which, table in enumerate((rel, srcidx)):
                for k in range(2):
                    act.wait_ge(s_rowsT_ps, 2 * which + k + 1)
                    cols = slice(k * CB * P, min(SC, (k + 1) * CB) * P)
                    act.copy(table[:, cols], bank[4 + 2 * which + k][:, 0:cols.stop - cols.start]).then_inc(s_rowsT, 1)
            act.wait_ge(s_rowsT, 4)
            act.copy(rel[:, STEPS_P:STEPS_P + G * RING], rel[:, 0:G * RING]).then_inc(s_rowsT, 1)
            act.copy(srcidx[:, STEPS_P:STEPS_P + G * RING], srcidx[:, 0:G * RING]).then_inc(s_rowsT, 1)
            act.wait_ge(s_shift, 2)
            for b in range(BLOCKS):
                act.activation(xn[:, b, :], x[:, b, :], ACT.Identity, bias=shift[:, b:b + 1], scale=rstd[:, b:b + 1]).then_inc(s_xn1, 1)
            act.wait_ge(s_degsum_ps, 1)
            act.activation(degstd[:], bank[3][:, 0:1], ACT.Sqrt, scale=1.0 / (N - 1)).then_inc(s_degstd, 1)

            def untranspose(l, which, c, gain=None, shift=None):
                t = TURN[l, which, c]
                act.wait_ge(s_tp, t + 1)
                source = bank[t % 2][:, 0:CHUNKS[c][1] * P]
                if gain is None:
                    act.copy(xnT[:, chunk_cols(c)], source).then_inc(s_xnT, 1)
                else:
                    act.activation(xnT[:, chunk_cols(c)], source, ACT.Identity, bias=w[l][:, shift:shift + 1], scale=w[l][:, gain:gain + 1]).then_inc(s_xnT, 1)

            def q_first(l, c):
                act.wait_ge(s_qkv, l * BLOCKS + CHUNKS[c][0] + CHUNKS[c][1])
                act.copy(chunk_blocks(qp[:, :, 0, :], c), chunk_blocks(qkv[:, :, 0:D], c)).then_inc(s_q1, 1)

            def q_second(l, c):
                act.wait_ge(s_r1, l * NCH + c + 1)
                act.copy(chunk_blocks(qp[:, :, 1, :], c), qres[:, c % 2, 0:CHUNKS[c][1], :]).then_inc(s_q2, 1)

            def edge_copy(l, g, r):
                n = l * GROUPS + g
                act.wait_ge(s_ohT_ps, n + 1)
                act.copy(onehotT[:, r % 2, :, :].rearrange("p j e -> p (j e)"), bank[r % 2][:].bitcast(BF16)[:, 0:G * P]).then_inc(s_ohT, 1)

            def edge_exp(l, g, r):
                n = l * GROUPS + g
                act.wait_ge(s_attc, n + 1)
                act.activation(msg[:, r % 2, :, D:AGG], attc[:, r % 2, :].rearrange("p (j h) -> p j h", h=H), ACT.Exp).then_inc(s_ex, 1)

            def edge_iteration(l, g, r):
                edge_exp(l, g, r)
                if given(g, 0, GROUPS - 2):
                    edge_copy(l, g + 2, (r + 2) % RING)

            def gelu(l, c):
                for f in range(FC):
                    act.wait_ge(s_ff1, (l * NCH + c) * FC + f + 1)
                    if c >= 2:
                        act.wait_ge(s_y_ps, l * NCH + c - 1)
                    n = CHUNKS[c][1] * P
                    act.activation(hT[:, c % 2, f, 0:n], bank[4 + f % 2][:, 0:n], ACT.Gelu, bias=w[l][:, V_FF + f:V_FF + f + 1]).then_inc(s_gelu, 1)

            def dense(post, pre):
                if post is None:
                    untranspose(pre, "ln1", 0, V_G1, V_B1)
                    for c in range(NCH + LAG_Q - LAG_LN1):
                        if c + 1 < NCH:
                            untranspose(pre, "ln1", c + 1, V_G1, V_B1)
                        if c >= LAG_Q - LAG_LN1:
                            q_first(pre, c - (LAG_Q - LAG_LN1))
                            q_second(pre, c - (LAG_Q - LAG_LN1))
                    return
                for i in slots(post, pre):
                    if pre is not None and 0 <= i - LAG_Q < NCH:
                        q_first(pre, i - LAG_Q)
                        q_second(pre, i - LAG_Q)
                    if post is not None and i < NCH:
                        untranspose(post, "out", i)
                    if post is not None and 0 <= i - LAG_LN2 < NCH:
                        untranspose(post, "ln2", i - LAG_LN2, V_G2, V_B2)
                    if post is not None and 0 <= i - LAG_W1 < NCH:
                        gelu(post, i - LAG_W1)
                    if pre is not None and 0 <= i - LAG_LN1 < NCH:
                        untranspose(pre, "ln1", i - LAG_LN1, V_G1, V_B1)

            act.wait_ge(s_w, 16 * (2 * L + 1))
            dense(None, 0)
            for l in range(L):
                act.wait_ge(s_loop_att, l + 1)
                act.activation(agg[:, :, D:AGG], loop_att[:].rearrange("p (b h) -> p b h", h=H), ACT.Exp).then_inc(s_loop_ex, 1)

                edge_copy(l, 0, 0)
                edge_copy(l, 1, 1)
                for g in range(RING):
                    edge_iteration(l, g, g)
                with act.Fori(1, ROUNDS - 1) as it:
                    for r in range(RING):
                        edge_iteration(l, it * RING + r, r)
                for r in range(RING):
                    edge_iteration(l, GROUPS - RING + r, r)

                dense(l, l + 1 if l + 1 < L else None)

        @program.vector
        def _(dve):
            links = [0]

            def link(instruction):
                links[0] += 1
                instruction.then_inc(s_chain, 1)
                dve.wait_ge(s_chain, links[0])

            dve.wait_ge(s_last, 16)
            link(dve.tensor_copy(last_f[:], last_i[:]))
            dve.wait_ge(s_const, STEP_CONSTS)
            link(dve.tensor_tensor(before[:], last_f[:].unsqueeze(1).broadcast_to([P, BLOCKS - 1, TC]), thr[:].unsqueeze(2).broadcast_to([P, BLOCKS - 1, TC]), ALU.is_lt))
            dve.tensor_reduce(count[:], before[:], AX, ALU.add).then_inc(s_count, 1)
            dve.wait_ge(s_first_ps, 1)
            link(dve.tensor_tensor(first[:], bank[0][:, 0:BLOCKS - 1], blockno[:], ALU.add))
            link(dve.tensor_tensor(begun[:], first[:].unsqueeze(1).broadcast_to([P, SC, BLOCKS - 1]), stepno[:].unsqueeze(2).broadcast_to([P, SC, BLOCKS - 1]), ALU.is_le))
            dve.tensor_reduce(block[:], begun[:], AX, ALU.add).then_inc(s_block, 1)
            dve.wait_ge(s_block, 1)
            link(dve.tensor_tensor(stepno[:], stepno[:], block[:], ALU.subtract))
            dve.tensor_scalar(tileno[:], stepno[:], float(TILES_P - 1), None, ALU.min).then_inc(s_tileno, 1)
            dve.tensor_scalar(block128[:], block[:], float(P), None, ALU.mult).then_inc(s_block128, 1)
            dve.wait_ge(s_blockT_ps, 1)
            dve.tensor_copy(blockT[:], bank[1][0:SC, 0:P]).then_inc(s_blockT, 1)

            dve.wait_ge(s_src, 16)
            dve.tensor_scalar(low_i, src_nat, LO - 1, None, ALU.bitwise_and).then_inc(s_digits_i, 1)
            dve.tensor_scalar(high_i, src_nat, LO.bit_length() - 1, None, ALU.logical_shift_right).then_inc(s_digits_i, 1)

            stats_done = [0]

            def norm_stats(c, source, s_var):
                b0, nb = CHUNKS[c]
                for b in range(b0, b0 + nb):
                    dve.bn_stats(stats[:, b, :], source[:, b, :]).then_inc(s_stats, 1)
                stats_done[0] += nb
                dve.wait_ge(s_stats, stats_done[0])
                for b in range(b0, b0 + nb):
                    dve.bn_aggr(mv[:, b, :], stats[:, b, :]).then_inc(s_var, 1)

            def normalise(c, s_rstd, chunks, s_done):
                dve.wait_ge(s_rstd, chunks)
                b0, nb = CHUNKS[c]
                for b in range(b0, b0 + nb):
                    dve.tensor_scalar(xn[:, b, :], x[:, b, :], mv[:, b, 0:1], rstd[:, b:b + 1], ALU.subtract, ALU.mult).then_inc(s_done, 1)

            def scale_and_shift(n):
                dve.wait_ge(s_std, n + 1)
                dve.reciprocal(rstd[:], std[:]).then_inc(s_rstd, 1)
                dve.wait_ge(s_rstd, n + 1)
                dve.scalar_tensor_tensor(out=shift[:], in0=mv[:, :, 0], scalar=-1.0, in1=rstd[:], op0=ALU.mult, op1=ALU.mult).then_inc(s_shift, 1)

            def hist_step(k, buf, t0):
                if k >= 2:
                    dve.wait_ge(s_hist_mm, k - 1)
                for oh, values, size in ((oh_low, low, LO), (oh_high, high, HI)):
                    ins = dve.tensor_tensor(oh[:, buf, :, :], digit[:, 0:size, :], values[:, bass.ds(t0, HT)].unsqueeze(1).broadcast_to([P, size, HT]), ALU.is_equal)
                ins.then_inc(s_hist_oh, 1)

            def input_mean():
                dve.wait_ge(s_sums_in, BLOCKS)
                dve.tensor_scalar(shift[:], x_sums[:, 0, :], -1.0 / D, None, ALU.mult).then_inc(s_mean_in, 1)
                dve.tensor_scalar(mv[:, :, 0], x_sums[:, 0, :], 1.0 / D, None, ALU.mult)

            def input_var():
                dve.wait_ge(s_sums_in, 2 * BLOCKS)
                dve.tensor_scalar(mv[:, :, 1], x_sums[:, 1, :], 1.0 / D, None, ALU.mult).then_inc(s_var_in, 1)

            def first_layer_var():
                dve.wait_ge(s_squares, BLOCKS)
                link(dve.tensor_scalar(x_sums[:], x_sums[:], 1.0 / D, None, ALU.mult))
                link(dve.tensor_tensor(shift[:], x_sums[:, 0, :], x_sums[:, 0, :], ALU.mult))
                dve.tensor_copy(mv[:, :, 0], x_sums[:, 0, :])
                dve.tensor_tensor(mv[:, :, 1], x_sums[:, 1, :], shift[:], ALU.subtract).then_inc(s_var1, BLOCKS)

            dve.wait_ge(s_const, CONSTS)
            dve.wait_ge(s_digits, 2)
            for k in range(HSTEPS):
                hist_step(k, k % 2, k * HT)
                if k == 2:
                    input_mean()
                elif k == 5:
                    input_var()
                elif k == 6:
                    scale_and_shift(0)
                elif k == HSTEPS - 4:
                    first_layer_var()
                elif k == HSTEPS - 3:
                    scale_and_shift(1)
            dve.wait_ge(s_hist_mm, HSTEPS)
            dve.scalar_tensor_tensor(out=deg[:], in0=bank[2][0:LO, 0:HI], scalar=1.0 - (E + N) / N, in1=valid[:], op0=ALU.add, op1=ALU.mult).then_inc(s_deg, 1)
            dve.wait_ge(s_deg, 1)
            link(dve.tensor_tensor(degsq[:], deg[:], deg[:], ALU.mult))
            dve.tensor_reduce(degsum[:], degsq[:], AX, ALU.add).then_inc(s_degsum, 1)
            dve.wait_ge(s_degT_ps, 1)
            dve.tensor_copy(degT[:], bank[2][0:HI, 0:LO]).then_inc(s_degT, 1)
            dve.wait_ge(s_w, 16 * (2 * L + 1))
            dve.wait_ge(s_degstd, 1)
            link(dve.tensor_scalar(degstd[:], degstd[:], 1e-6, None, ALU.add))
            link(dve.reciprocal(degstd[:], degstd[:]))
            dve.tensor_scalar(wdeg[:], wdeg[:], degstd[0:1, :], None, ALU.mult).then_inc(s_wdeg, 1)

            for l in range(L):
                link(dve.tensor_tensor(pos_bias[:, l:l + 1], w[l][:, V_POS:V_POS + 1], w[l][:, V_DEG:V_DEG + 1], ALU.add))
                link(dve.tensor_scalar(w[l][:, W_QKV:W_QKV + D], w[l][:, W_QKV:W_QKV + D], HD ** -0.5, None, ALU.mult))
                link(dve.tensor_scalar(row[l][:, R_QKV:R_QKV + D], row[l][:, R_QKV:R_QKV + D], HD ** -0.5, None, ALU.mult))

            def position(l, c):
                dve.wait_ge(s_xp_ps, l * NCH + c + 1)
                cols = chunk_cols(c)
                dve.scalar_tensor_tensor(out=xnT[:, cols], in0=pos_bank(l, c)[:, 0:CHUNKS[c][1] * P], scalar=pos_bias[:, l:l + 1],
                                         in1=xnT[:, cols], op0=ALU.add, op1=ALU.add).then_inc(s_xpT, 1)

            def qkv_bias(l, c):
                b0, nb = CHUNKS[c]
                for b in range(b0, b0 + nb):
                    dve.wait_ge(s_qkv_ps, l * BLOCKS + b + 1)
                    dve.tensor_tensor(qkv[:, b, :], project_bank(l, b)[:, 0:3 * D], row[l][:, R_QKV:R_QKV + 3 * D], ALU.add).then_inc(s_qkv, 1)

            def q_rest(l, c):
                dve.wait_ge(s_q1, l * NCH + c + 1)
                if l or c >= 2:
                    dve.wait_ge(s_q3, l * NCH + c - 1)
                dve.tensor_tensor(qres[:, c % 2, 0:CHUNKS[c][1], :], chunk_blocks(qkv[:, :, 0:D], c), chunk_blocks(qp[:, :, 0, :], c), ALU.subtract).then_inc(s_r1, 1)

            def q_third(l, c):
                dve.wait_ge(s_q2, l * NCH + c + 1)
                dve.tensor_tensor(chunk_blocks(qp[:, :, 2, :], c), qres[:, c % 2, 0:CHUNKS[c][1], :], chunk_blocks(qp[:, :, 1, :], c), ALU.subtract).then_inc(s_q3, 1)

            def by_head(t):
                return t.rearrange("p b (h d) -> p b h d", d=HD)

            def self_loops(l):
                dve.wait_ge(s_qkv, (l + 1) * BLOCKS)
                link(dve.tensor_tensor(xn[:], qkv[:, :, 0:D], qkv[:, :, D:2 * D], ALU.mult))
                link(dve.tensor_reduce(loop_att[:], xn[:].rearrange("p b (h d) -> p (b h) d", d=HD), AX, ALU.add))
                link(dve.tensor_tensor(loop_nan[:], loop_att[:], loop_att[:], ALU.not_equal))
                link(dve.tensor_scalar(loop_att[:], loop_att[:], -50.0, 50.0, ALU.max, ALU.min))
                dve.copy_predicated(loop_att[:], loop_nan[:], zeros[:]).then_inc(s_loop_att, 1)
                dve.wait_ge(s_loop_ex, l + 1)
                dve.tensor_tensor(by_head(agg[:, :, 0:D]), by_head(qkv[:, :, 2 * D:3 * D]),
                                  agg[:, :, D:AGG].unsqueeze(3).broadcast_to([P, BLOCKS, H, HD]), ALU.mult).then_inc(s_agg0, 1)
                dve.wait_ge(s_agg0, l + 1)

            def attention_norm(l, c):
                b0, nb = CHUNKS[c]
                dve.reciprocal(rsum[:, b0:b0 + nb, :], agg[:, b0:b0 + nb, D:AGG]).then_inc(s_rsum, 1)
                dve.wait_ge(s_rsum, l * NCH + c + 1)
                dve.tensor_tensor(by_head(chunk_blocks(xn, c)), by_head(chunk_blocks(agg[:, :, 0:D], c)),
                                  rsum[:, b0:b0 + nb, :].unsqueeze(3).broadcast_to([P, nb, H, HD]), ALU.mult).then_inc(s_norm, 1)

            def add_to_x(l, c, which, s_product, s_done):
                dve.wait_ge(s_product, l * NCH + c + 1)
                dve.tensor_tensor(chunk_blocks(x, c), chunk_blocks(x, c), chunk_bank(which, c), ALU.add).then_inc(s_done, 1)

            def dense(post, pre):
                if post is not None:
                    attention_norm(post, 0)
                for i in slots(post, pre):
                    if post is not None and 0 <= i - LAG_LN2 < NCH:
                        normalise(i - LAG_LN2, s_rstd2, post * NCH + i - LAG_LN2 + 1, s_xn2)
                    if pre is not None and 0 <= i - LAG_QKV < NCH:
                        position(pre, i - LAG_QKV)
                    if pre is not None and 0 <= i - LAG_Q < NCH:
                        q_rest(pre, i - LAG_Q)
                    if post is not None and i + 1 < NCH:
                        attention_norm(post, i + 1)
                    if pre is not None and 0 <= i - LAG_Q < NCH:
                        q_third(pre, i - LAG_Q)
                    if post is not None and 0 <= i - LAG_W2 < NCH:
                        c = i - LAG_W2
                        if post == L - 1:
                            dve.wait_ge(s_x0, c + 1)
                        else:
                            dve.wait_ge(s_b2, post * NCH + c + 1)
                        add_to_x(post, c, 3, s_y_ps, s_y)
                        if pre is not None:
                            dve.wait_ge(s_y, post * NCH + c + 1)
                            norm_stats(c, x, s_var1)
                    if post is not None and i < NCH:
                        dve.wait_ge(s_bo, post + 1)
                        add_to_x(post, i, 2, s_o_ps, s_o)
                        dve.wait_ge(s_o, post * NCH + i + 1)
                        norm_stats(i, x, s_var2)
                    if post is not None and pre is not None and 0 <= i - LAG_LN1 < NCH:
                        normalise(i - LAG_LN1, s_rstd1, post * NCH + i - LAG_LN1 + 1, s_xn1)
                    if pre is not None and 0 <= i - LAG_QKV < NCH:
                        qkv_bias(pre, i - LAG_QKV)

            def edge_onehot(l, g, r):
                dve.tensor_tensor(onehot[:, r, :, :], iota_free[:].unsqueeze(1).broadcast_to([P, G, P]),
                                  rel[:, bass.ds(g * G, G)].unsqueeze(2).broadcast_to([P, G, P]), ALU.is_equal).then_inc(s_oh, 1)

            def edge_stage(g, r):
                dve.tensor_copy(idx[:, r, :], srcidx[:, bass.ds(g * G, G)]).then_inc(s_idx[r], 1)

            def edge_prod(l, g, r, kv_round):
                n = l * GROUPS + g
                skipped = PADS * l if r == RING - 1 else 0
                if isinstance(g, int) and g == GROUPS - 1:
                    skipped += PADS
                dve.wait_ge(s_kv[r], 16 * G * kv_round - 16 * skipped)
                dve.wait_ge(s_qe, n + 1)
                dve.tensor_tensor(prod[:], kvr[:, r, :, 0:D], bank[2 + r % 2][:].rearrange("p (j c) -> p j c", c=D), ALU.mult).then_inc(s_prod, 1)

            def edge_att(l, g, r):
                n = l * GROUPS + g
                dve.wait_ge(s_prod, n + 1)
                dve.tensor_reduce(att[:, r % 2, :], prod[:].rearrange("p j (h d) -> p (j h) d", d=HD), AX, ALU.add).then_inc(s_att, 1)

            def edge_clip(l, g, r):
                n = l * GROUPS + g
                dve.wait_ge(s_att, n + 1)
                dve.tensor_tensor(attnan[:, r % 2, :], att[:, r % 2, :], att[:, r % 2, :], ALU.not_equal)
                dve.tensor_scalar(attc[:, r % 2, :], att[:, r % 2, :], -50.0, 50.0, ALU.max, ALU.min).then_inc(s_clip, 1)

            def edge_guard(l, g, r):
                dve.copy_predicated(attc[:, r % 2, :], attnan[:, r % 2, :], zeros[:, 0:G * H]).then_inc(s_attc, 1)

            def edge_msg(l, g, r):
                n = l * GROUPS + g
                dve.wait_ge(s_ex, n + 1)
                dve.tensor_tensor(by_head(msg[:, r % 2, :, 0:D]), by_head(kvr[:, r, :, D:KV]),
                                  msg[:, r % 2, :, D:AGG].unsqueeze(3).broadcast_to([P, G, H, HD]), ALU.mult).then_inc(s_msg, 1)

            def edge_add(g, r, j, blocks):
                target = agg[:, bass.ds(blocks[j], 1), :].rearrange("p a c -> p (a c)")
                dve.tensor_tensor(target, target, agg_bank(r, j), ALU.add).then_inc(s_agg, 1)

            def edge_iteration(l, g, r, kv_round):
                n = l * GROUPS + g
                back, older = (r - 1) % RING, (r - 2) % RING
                adds = given(g, 2)
                blocks = read_blocks(ENG.DVE, g - 2) if adds else None

                def add(j):
                    if adds:
                        if j == 0:
                            dve.wait_ge(s_agg_ps, n - 1)
                        else:
                            dve.wait_ge(s_agg, (n - 2) * G + j)
                        edge_add(g - 2, older, j, blocks)

                if given(g, 3):
                    dve.wait_ge(s_agg, (n - 2) * G)
                edge_prod(l, g, r, kv_round)
                add(0)
                if given(g, 1):
                    edge_msg(l, g - 1, back)
                add(1)
                edge_att(l, g, r)
                if given(g, 1):
                    dve.wait_ge(s_msg, n)
                    edge_stage(g - 1 + RING, back)
                add(2)
                edge_clip(l, g, r)
                add(3)
                dve.wait_ge(s_clip, n + 1)
                edge_onehot(l, g + 2, (r + 2) % RING)
                edge_guard(l, g, r)

            dve.wait_ge(s_rowsT, 6)
            for r in range(RING):
                edge_stage(r, r)
            edge_onehot(0, 0, 0)
            edge_onehot(0, 1, 1)
            dense(None, 0)
            for l in range(L):
                self_loops(l)

                for g in range(RING):
                    edge_iteration(l, g, g, l * ROUNDS + 1)
                with dve.Fori(0, (ROUNDS - 2) // 2) as it:
                    for u in (1, 2):
                        for r in range(RING):
                            edge_iteration(l, it * (2 * RING) + (u * RING + r), r, it * 2 + (l * ROUNDS + u + 1))
                for r in range(RING):
                    edge_iteration(l, GROUPS - RING + r, r, (l + 1) * ROUNDS)
                last_blocks = [read_blocks(ENG.DVE, g) for g in (GROUPS - 2, GROUPS - 1)]
                edge_msg(l, GROUPS - 1, RING - 1)
                for g, blocks in zip((GROUPS - 2, GROUPS - 1), last_blocks):
                    dve.wait_ge(s_agg_ps, l * GROUPS + g + 1)
                    for j in range(G):
                        dve.wait_ge(s_agg, (l * GROUPS + g) * G + j)
                        edge_add(g, g % RING, j, blocks)
                dve.wait_ge(s_msg, (l + 1) * GROUPS)
                edge_stage(GROUPS - 1 + RING, RING - 1)

                dve.wait_ge(s_agg, (l + 1) * STEPS_P)
                dense(l, l + 1 if l + 1 < L else None)


OUT_SHAPE = (N, D)


def kernel(**inputs):
    import concourse.bacc as bacc
    from concourse.bass_utils import run_bass_kernel_spmd

    def get(name):
        return np.asarray(inputs["L0_gnn_" + name])

    x_pad = np.concatenate([np.asarray(inputs["x"]), np.zeros((NP - N, D), np.float32)])
    pad = TILES_P * P - E
    src_tiles = np.concatenate([np.asarray(inputs["src"]), np.full(pad, NP - 1, np.int32)]).reshape(TILES_P, P)
    dst_tiles = np.concatenate([np.asarray(inputs["dst"]), np.full(pad, NP, np.int32)]).reshape(TILES_P, P)
    src_flat = np.concatenate([np.asarray(inputs["src"]), np.full(HE * P - E, NP - 1, np.int32)]).reshape(P, HE)
    dst_last = np.full((TC * P,), NP, np.int32)
    dst_last[:TILES_P] = dst_tiles[:, P - 1]
    dst_last = np.ascontiguousarray(dst_last.reshape(TC, P).T)
    weights = np.concatenate(
        [get("Wpos"), get("Wq"), get("Wk"), get("Wv"), get("Wo"), get("W1"),
         get("W2").reshape(L, FC, P, D).transpose(0, 2, 1, 3).reshape(L, P, FC * D)]
        + [get(v)[:, :, None] for v in ("ln1_g", "ln1_b", "ln2_g", "ln2_b", "bpos", "bdeg")]
        + [get("b1").reshape(L, FC, P).transpose(0, 2, 1)], axis=2)
    rows = np.concatenate([get(v) for v in ("bq", "bk", "bv", "bo", "b2")], axis=1)
    wdeg = get("Wdeg").reshape(1, L, D)
    arrays = {"x_in": x_pad, "src_flat": src_flat, "src_tiles": src_tiles, "dst_tiles": dst_tiles, "dst_last": dst_last,
              "weights": weights, "rows": rows, "wdeg_in": wdeg}
    arrays = {k: np.ascontiguousarray(a) for k, a in arrays.items()}

    nc = bacc.Bacc("TRN2", target_bir_lowering=False, num_devices=1)
    args = {k: nc.dram_tensor(k, a.shape, mybir.dt.from_np(a.dtype), kind="ExternalInput").ap() for k, a in arrays.items()}
    out = nc.dram_tensor("out", OUT_SHAPE, F32, kind="ExternalOutput").ap()
    build(nc, out=out, **args)
    result = run_bass_kernel_spmd(nc, [arrays], core_ids=[0])
    return result.results[0]["out"]
```
